# Optimizing a Trainium2 kernel written in Bass

```python
import numpy as np
import jax
import jax.numpy as jnp

def _softmax(x, axis=-1):
    return jax.nn.softmax(x, axis=axis)

def _gelu(x):
    return jax.nn.gelu(x, approximate=True)

def _silu(x):
    return jax.nn.silu(x)

def _sigmoid(x):
    return jax.nn.sigmoid(x)

def _layernorm(x, axis=-1, eps=1e-05):
    m = jnp.mean(x, axis=axis, keepdims=True)
    v = jnp.var(x, axis=axis, keepdims=True)
    return (x - m) / jnp.sqrt(v + eps)

def _scatter_add(tgt, idx, src, axis=0):
    return tgt.at[idx].add(src)

def _segment_sum(src, seg, n):
    return jax.ops.segment_sum(src, seg, n)
kernel_name = 'mk_seq_preln_d1_jaxref_r8_e2702b'

def setup_inputs(seed: int=0):
    np.random.seed(seed)
    _w = jnp.asarray

    def _L0_attn_setup():
        import jax, jax.numpy as jnp
        import numpy as np
        B, L, DM = (2, 256, 256)
        EXPAND, D_STATE, D_CONV, H, CS = (2, 128, 4, 32, 32)
        D_INNER = EXPAND * DM
        HD = D_INNER // H
        N = D_STATE
        PROJ = 2 * D_INNER + 2 * H * N + H
        key = jax.random.key(seed)
        ks = jax.random.split(key, 8)
        x = jax.random.normal(ks[0], (B, L, DM), jnp.float32)
        W_in = jax.random.normal(ks[1], (PROJ, DM), jnp.float32) * 0.02
        conv_w = jax.random.normal(ks[2], (D_INNER, 1, D_CONV), jnp.float32) * 0.2
        conv_b = jnp.zeros((D_INNER,), jnp.float32)
        A_log = jnp.full((H,), jnp.log(2.0), jnp.float32)
        D_param = jnp.ones((D_INNER,), jnp.float32)
        dt_bias = jnp.zeros((H,), jnp.float32)
        W_out = jax.random.normal(ks[3], (DM, D_INNER), jnp.float32) * 0.02
        return {'x': x, 'W_in': W_in, 'conv_w': conv_w, 'conv_b': conv_b, 'A_log': A_log, 'D_param': D_param, 'dt_bias': dt_bias, 'W_out': W_out}
    _L0_attn_in = _L0_attn_setup()

    def _L0_ffn_setup():
        import jax, jax.numpy as jnp
        import numpy as np
        NUM_EXPERTS = 8
        TOP_K = 2
        LORA_ALPHA = 2.0
        LORA_RANK = 16
        D_MODEL = 256
        D_HIDDEN = 704
        key = jax.random.key(seed)
        ks = jax.random.split(key, 11)
        B, S, D, H, E, R = (2, 128, D_MODEL, D_HIDDEN, NUM_EXPERTS, LORA_RANK)
        sd = 1.0 / np.sqrt(D)
        sh = 1.0 / np.sqrt(H)
        x = jax.random.normal(ks[0], (B, S, D), jnp.float32)
        gate_w = jax.random.normal(ks[1], (E, D), jnp.float32) * sd
        w_up = jax.random.normal(ks[2], (H, D), jnp.float32) * sd
        w_gate = jax.random.normal(ks[3], (H, D), jnp.float32) * sd
        w_down = jax.random.normal(ks[4], (D, H), jnp.float32) * sh
        up_A = jax.random.normal(ks[5], (E, R, D), jnp.float32) * sd
        up_B = jax.random.normal(ks[6], (E, H, R), jnp.float32) * 0.02
        gate_A = jax.random.normal(ks[7], (E, R, D), jnp.float32) * sd
        gate_B = jax.random.normal(ks[8], (E, H, R), jnp.float32) * 0.02
        down_A = jax.random.normal(ks[9], (E, R, H), jnp.float32) * sh
        down_B = jax.random.normal(ks[10], (E, D, R), jnp.float32) * 0.02
        return {'x': x, 'gate_w': gate_w, 'w_up': w_up, 'w_gate': w_gate, 'w_down': w_down, 'up_A': up_A, 'up_B': up_B, 'gate_A': gate_A, 'gate_B': gate_B, 'down_A': down_A, 'down_B': down_B}
    _L0_ffn_in = _L0_ffn_setup()
    _d = {'L0_attn_x': _L0_attn_in['x'], 'L0_attn_W_in': _L0_attn_in['W_in'], 'L0_attn_conv_w': _L0_attn_in['conv_w'], 'L0_attn_conv_b': _L0_attn_in['conv_b'], 'L0_attn_A_log': _L0_attn_in['A_log'], 'L0_attn_D_param': _L0_attn_in['D_param'], 'L0_attn_dt_bias': _L0_attn_in['dt_bias'], 'L0_attn_W_out': _L0_attn_in['W_out'], 'L0_ffn_gate_w': _L0_ffn_in['gate_w'], 'L0_ffn_w_up': _L0_ffn_in['w_up'], 'L0_ffn_w_gate': _L0_ffn_in['w_gate'], 'L0_ffn_w_down': _L0_ffn_in['w_down'], 'L0_ffn_up_A': _L0_ffn_in['up_A'], 'L0_ffn_up_B': _L0_ffn_in['up_B'], 'L0_ffn_gate_A': _L0_ffn_in['gate_A'], 'L0_ffn_gate_B': _L0_ffn_in['gate_B'], 'L0_ffn_down_A': _L0_ffn_in['down_A'], 'L0_ffn_down_B': _L0_ffn_in['down_B']}
    _x0 = _d['L0_attn_x']
    _d['L0_attn_x'] = jax.random.normal(jax.random.fold_in(jax.random.key(seed), 1), (16, 256, 256), dtype=_x0.dtype)
    del _x0
    return _d

def reference(L0_attn_x, L0_attn_W_in, L0_attn_conv_w, L0_attn_conv_b, L0_attn_A_log, L0_attn_D_param, L0_attn_dt_bias, L0_attn_W_out, L0_ffn_gate_w, L0_ffn_w_up, L0_ffn_w_gate, L0_ffn_w_down, L0_ffn_up_A, L0_ffn_up_B, L0_ffn_gate_A, L0_ffn_gate_B, L0_ffn_down_A, L0_ffn_down_B):

    def _L0_attn_ref(x, W_in, conv_w, conv_b, A_log, D_param, dt_bias, W_out):
        import jax, jax.numpy as jnp
        import numpy as np
        B, L, DM = (2, 256, 256)
        EXPAND, D_STATE, D_CONV, H, CS = (2, 128, 4, 32, 32)
        D_INNER = EXPAND * DM
        HD = D_INNER // H
        N = D_STATE
        PROJ = 2 * D_INNER + 2 * H * N + H
        b, l, _ = x.shape
        proj = x @ W_in.T
        val, gate, Bp, Cp, dt = jnp.split(proj, [D_INNER, 2 * D_INNER, 2 * D_INNER + H * N, 2 * D_INNER + 2 * H * N], axis=-1)
        vc = jax.lax.conv_general_dilated(val.transpose(0, 2, 1), conv_w, (1,), [(D_CONV - 1, 0)], dimension_numbers=('NCH', 'OIH', 'NCH'), feature_group_count=D_INNER)
        val = jax.nn.silu(vc.transpose(0, 2, 1) + conv_b)
        val = val.reshape(b, l, H, HD)
        Bp = Bp.reshape(b, l, H, N)
        Cp = Cp.reshape(b, l, H, N)
        dt = jax.nn.softplus(dt + dt_bias)
        ld = dt * -jnp.exp(A_log)
        nC = l // CS
        mask = jnp.tril(jnp.ones((CS, CS), bool))
        Dh = D_param.reshape(1, H, 1, HD)

        def chunk(h, inp):
            val_c, B_c, C_c, ld_c = inp
            cum = jnp.cumsum(ld_c, axis=1)
            cumh = cum.transpose(0, 2, 1)
            diff = jnp.where(mask, cumh[:, :, :, None] - cumh[:, :, None, :], -jnp.inf)
            CB = jnp.einsum('blhn,bmhn->bhlm', C_c, B_c)
            M = CB * jnp.exp(diff)
            val_ch = val_c.transpose(0, 2, 1, 3)
            Y = M @ val_ch + jnp.einsum('blhn,bhdn,blh->bhld', C_c, h, jnp.exp(cum)) + Dh * val_ch
            last = cum[:, -1, :]
            h_new = jnp.exp(last)[:, :, None, None] * h + jnp.einsum('blhd,blhn,blh->bhdn', val_c, B_c, jnp.exp(last[:, None, :] - cum))
            return (h_new, Y)
        inps = tuple((jnp.moveaxis(a.reshape(b, nC, CS, *a.shape[2:]), 1, 0) for a in (val, Bp, Cp, ld)))
        h0 = jnp.zeros((b, H, HD, N), jnp.float32)
        _, Ys = jax.lax.scan(chunk, h0, inps)
        Y = Ys.transpose(1, 0, 3, 2, 4).reshape(b, l, D_INNER)
        Y = Y * jax.nn.silu(gate)
        return Y @ W_out.T

    def _L0_ffn_ref(x, gate_w, w_up, w_gate, w_down, up_A, up_B, gate_A, gate_B, down_A, down_B):
        import jax, jax.numpy as jnp
        import numpy as np
        NUM_EXPERTS = 8
        TOP_K = 2
        LORA_ALPHA = 2.0
        LORA_RANK = 16
        D_MODEL = 256
        D_HIDDEN = 704
        B, S, D = x.shape
        H = w_up.shape[0]
        gate_logits = jnp.einsum('bsd,ed->bse', x, gate_w)
        topw, sel = jax.lax.top_k(gate_logits, TOP_K)
        topw = jax.nn.softmax(topw.astype(jnp.float32), axis=1).astype(x.dtype)
        xt = x.reshape(-1, D)
        wf = topw.reshape(-1, TOP_K)
        sf = sel.reshape(-1, TOP_K)
        base_up = xt @ w_up.T
        base_gate = xt @ w_gate.T
        mixed_h = jnp.zeros((xt.shape[0], H), x.dtype)
        lora_down = jnp.zeros_like(xt)
        for e in range(NUM_EXPERTS):
            c = jnp.sum(jnp.where(sf == e, wf, 0.0), axis=1)
            lo_up = LORA_ALPHA * (xt @ up_A[e].T @ up_B[e].T)
            lo_gate = LORA_ALPHA * (xt @ gate_A[e].T @ gate_B[e].T)
            h_e = jax.nn.silu(base_up + lo_up) * (base_gate + lo_gate)
            ch = c[:, None] * h_e
            mixed_h = mixed_h + ch
            lora_down = lora_down + LORA_ALPHA * (ch @ down_A[e].T @ down_B[e].T)
        out = mixed_h @ w_down.T + lora_down
        return out.reshape(B, S, D)
    x = L0_attn_x
    x = x + _L0_attn_ref(_layernorm(x, axis=-1), L0_attn_W_in, L0_attn_conv_w, L0_attn_conv_b, L0_attn_A_log, L0_attn_D_param, L0_attn_dt_bias, L0_attn_W_out)
    x = x + _L0_ffn_ref(_layernorm(x, axis=-1), L0_ffn_gate_w, L0_ffn_w_up, L0_ffn_w_gate, L0_ffn_w_down, L0_ffn_up_A, L0_ffn_up_B, L0_ffn_gate_A, L0_ffn_gate_B, L0_ffn_down_A, L0_ffn_down_B)
    return x

_drawn_inputs = setup_inputs


def setup_inputs(seed=0):
    import zlib

    import numpy as np

    out = dict(_drawn_inputs(seed))
    spreads = {'L0_attn_conv_b': (0.0, 0.8),
     'L0_attn_A_log': (0.6931471824645996, 0.6),
     'L0_attn_D_param': (1.0, 0.6),
     'L0_attn_dt_bias': (0.0, 0.8)}
    factors = {'L0_attn_W_in': 5.335,
     'L0_attn_conv_w': 6.304,
     'L0_attn_W_out': 4.986,
     'L0_ffn_gate_w': 8.0,
     'L0_ffn_w_up': 8.0,
     'L0_ffn_w_gate': 8.0,
     'L0_ffn_w_down': 7.932,
     'L0_ffn_up_A': 8.0,
     'L0_ffn_up_B': 8.0,
     'L0_ffn_gate_A': 8.0,
     'L0_ffn_gate_B': 8.0,
     'L0_ffn_down_A': 8.0,
     'L0_ffn_down_B': 8.0}
    for name, (base, spread) in spreads.items():
        noise = np.random.default_rng([zlib.crc32(name.encode()), seed]).standard_normal(out[name].shape)
        drawn = base * np.exp(spread * noise) if base else spread * noise
        out[name] = jnp.asarray(drawn.astype(out[name].dtype))
    for name, factor in factors.items():
        out[name] = (out[name] * factor).astype(out[name].dtype)
    return out
```

```python
from contextlib import ExitStack

import concourse.bass as bass
from concourse import mybir

F32 = mybir.dt.float32
F32R = mybir.dt.float32r
ACT = mybir.ActivationFunctionType
ALU = mybir.AluOpType
AX_X = mybir.AxisListType.X

P = 128
SEQS, SEQ, DM = 16, 256, 256
TOK = SEQS * SEQ
TILES = TOK // P
KT = DM // P
H, HD, N = 32, 16, 128
DI = H * HD
CT = DI // P
TAPS = 4
GH = 4
GROUPS = H // GH
GCH = GH * HD
CPS = SEQ // P
BLK = 512
NBLK = TOK // BLK
TPB = BLK // P
E, R = 8, 16
HID = 704
HT = (HID + P - 1) // P
HROWS = [min(P, HID - t * P) for t in range(HT)]
EPS = 1e-5
LORA_ALPHA = 2.0
NEG = -1.0e30


def f32(ap):
    return ap.bitcast(F32)


class Scope:

    over = []

    def __init__(self, nc, ctx, stage):
        self.nc, self.ctx, self.stage = nc, ctx, stage

    def sb(self, name, shape, dt=F32):
        return self.ctx.enter_context(self.nc.sbuf_tensor(f"{self.stage}_{name}", shape, dt))

    def bank(self, name):
        return self.ctx.enter_context(self.nc.psum_tensor(f"{self.stage}_{name}", [P, 512], F32))

    def sem(self, name):
        made = self.nc.alloc_semaphore(f"{self.stage}_{name}")
        self.over.append(made)
        return made


def three_passes(pe, out, wh, wl, xh, xl, start, stop, skip=False):
    pe.matmul(out, wh, xh, start=start, stop=False, skip_group_check=skip)
    pe.matmul(out, wh, xl, start=False, stop=False, skip_group_check=skip)
    return pe.matmul(out, wl, xh, start=False, stop=stop, skip_group_check=skip)


def at_least(eng, sem, value):
    if not isinstance(value, int) or value > 0:
        eng.wait_ge(sem, value)


def finish_moments(v, st, mean, rstd, stats_done, step, var_ready, root_done, rstd_done):
    v.wait_ge(stats_done, TILES)
    v.tensor_tensor(mean[:], st[:, :, 1], st[:, :, 4], ALU.add).then_inc(step, 1)
    v.tensor_tensor(rstd[:], st[:, :, 1], st[:, :, 4], ALU.subtract).then_inc(step, 1)
    v.wait_ge(step, 2)
    v.tensor_scalar(mean[:], mean[:], 0.5, None, ALU.mult).then_inc(step, 1)
    v.scalar_tensor_tensor(rstd[:], rstd[:], 0.25, rstd[:], ALU.mult, ALU.mult).then_inc(step, 1)
    v.tensor_tensor(st[:, :, 0], st[:, :, 2], st[:, :, 5], ALU.add).then_inc(step, 1)
    v.wait_ge(step, 5)
    v.scalar_tensor_tensor(rstd[:], st[:, :, 0], 1.0 / DM, rstd[:], ALU.mult, ALU.add).then_inc(step, 1)
    v.wait_ge(step, 6)
    v.tensor_scalar(rstd[:], rstd[:], EPS, None, ALU.add).then_inc(var_ready, 1)
    v.wait_ge(root_done, 1)
    v.reciprocal(rstd[:], rstd[:]).then_inc(rstd_done, 1)
    v.wait_ge(rstd_done, 1)


def stage_load_and_moments(nc, d, keep):
    with ExitStack() as ctx:
        sc = Scope(nc, ctx, "ln1")
        x_sb, mean, rstd = keep["x"], keep["mean"], keep["rstd"]
        st = sc.sb("st", [P, TILES, 6])
        x_in = [sc.sem(f"x_in{c}") for c in range(8)]
        stats_done, step, var_ready, root_done, rstd_done = (
            sc.sem(n) for n in ("stats_done", "step", "var_ready", "root_done", "rstd_done"))
        block = ctx.enter_context(nc.Block())

        @block.sync
        def _(sp):
            xv = d["x"].rearrange("s (c p) d -> p (s c) d", p=P)
            for c in range(8):
                sp.dma_start(x_sb[:, 4 * c:4 * c + 4, :], xv[:, 4 * c:4 * c + 4, :]).then_inc(x_in[c], 16)

        @block.vector
        def _(v):
            for c in range(8):
                v.wait_ge(x_in[c], 16)
                for t in range(4 * c, 4 * c + 4):
                    v.bn_stats(st[:, t, :], x_sb[:, t, :]).then_inc(stats_done, 1)
            finish_moments(v, st, mean, rstd, stats_done, step, var_ready, root_done, rstd_done)

        @block.scalar
        def _(act):
            act.wait_ge(var_ready, 1)
            act.activation(rstd[:], rstd[:], ACT.Sqrt).then_inc(root_done, 1)


def stage_values(nc, d, keep):
    with ExitStack() as ctx:
        sc = Scope(nc, ctx, "val")
        x_sb, mean, rstd, xh, xl, dt_raw = (keep[n] for n in ("x", "mean", "rstd", "xh", "xl", "dt"))
        w_raw = sc.sb("w_raw", [P, KT, DI + P])
        w_h, w_l = (sc.sb(n, [P, KT, DI + P], F32R) for n in ("w_h", "w_l"))
        taps = sc.sb("taps", [P, CT, TAPS])
        conv_b = sc.sb("conv_b", [P, CT])
        dt_bias = sc.sb("dt_bias", [H, 1])
        ident = sc.sb("ident", [P, P])
        xn = [sc.sb(f"xn{k}", [P, CPS, DM]) for k in range(2)]
        vbuf = [sc.sb(f"vbuf{k}", [P, CT, TAPS - 1 + SEQ]) for k in range(2)]
        acc = [sc.sb(f"acc{k}", [P, CT, SEQ]) for k in range(2)]
        vs = [sc.sb(f"vs{k}", [P, CT, SEQ]) for k in range(2)]
        vtok = [sc.sb(f"vtok{k}", [P, CPS, DI]) for k in range(2)]
        ps_t = [sc.bank(f"ps_t{k}") for k in range(2)]
        ps_v = [sc.bank(f"ps_v{k}") for k in range(2)]
        ps_dt = sc.bank("ps_dt")
        ps_o = [sc.bank(f"ps_o{k}") for k in range(2)]
        small_in, w_in, w_hi, w_lo, pad_ready = (
            sc.sem(n) for n in ("small_in", "w_in", "w_hi", "w_lo", "pad_ready"))
        xn_ready, tr_done, xhi_done, xlo_done = (
            sc.sem(n) for n in ("xn_ready", "tr_done", "xhi_done", "xlo_done"))
        v_done, v_evac, dt_done, dt_evac, conv_step, silu_done = (
            sc.sem(n) for n in ("v_done", "v_evac", "dt_done", "dt_evac", "conv_step", "silu_done"))
        vt_done, vtok_c0, vtok_c1 = (sc.sem(n) for n in ("vt_done", "vtok_c0", "vtok_c1"))
        vT_out = [sc.sem(f"vT_out{k}") for k in range(2)]
        vtok_out = [sc.sem(f"vtok_out{k}") for k in range(2)]
        STEPS = CT * (TAPS - 1)
        block = ctx.enter_context(nc.Block())

        def slots(eng, slot):
            for s in range(4):
                slot(s, s % 2)
            with eng.Fori(2, SEQS // 2 - 1) as q:
                for k in range(2):
                    slot(q * 2 + k, k)
            for s in range(SEQS - 2, SEQS + 2):
                slot(s, s % 2)

        def live(n):
            return not isinstance(n, int) or 0 <= n < SEQS

        def starts(s):
            return not isinstance(s, int) or s < SEQS

        @block.sync
        def _(sp):
            sp.dma_start(w_raw[:, :, 0:DI], d["w_val"]).then_inc(w_in, 16)
            sp.dma_start(w_raw[:, :, DI:DI + H], d["w_dt"]).then_inc(w_in, 16)
            for dst, src in ((taps, "taps"), (conv_b, "conv_b"), (dt_bias, "dt_bias"), (ident, "ident")):
                sp.dma_start(dst[:], d[src]).then_inc(small_in, 16)

            vT_view = d["vT"].rearrange("(c p) l -> p c l", p=P)

            def slot(s, k):
                m = s - 2
                if live(m):
                    sp.wait_ge(silu_done, m + 1)
                    sp.dma_start(vT_view[:, :, bass.ds(m * SEQ, SEQ)], vs[k][:]).then_inc(vT_out[k], 16)
                    sp.wait_ge(vtok_c0, m + 1)
                    sp.wait_ge(vtok_c1, m + 1)
                    for c in range(CPS):
                        sp.dma_start(d["val"][bass.ds(m, 1), :, :, c, :].rearrange("s g p q -> p (s g) q"),
                                     vtok[k][:, c, :].rearrange("p (g q) -> p g q", q=GCH)
                                     ).then_inc(vtok_out[k], 16)
            slots(sp, slot)
            for k in range(2):
                sp.wait_ge(vT_out[k], 16 * (SEQS // 2))
                sp.wait_ge(vtok_out[k], 32 * (SEQS // 2))

        @block.gpsimd
        def _(pool):
            pool.memset(w_raw[:, :, DI + H:], 0.0).then_inc(pad_ready, 1)
            for k in range(2):
                pool.memset(vbuf[k][:, :, 0:TAPS - 1], 0.0).then_inc(pad_ready, 1)

        @block.tensor
        def _(pe):
            pe.wait_ge(small_in, 64)

            def slot(s, k):
                n, m = s - 1, s - 2
                if starts(s):
                    at_least(pe, xlo_done, s - 1)
                    pe.wait_ge(xn_ready, s + 1)
                    for kt in range(KT):
                        for c in range(CPS):
                            last = pe.transpose(ps_t[k][:, kt * SEQ + c * P:kt * SEQ + (c + 1) * P],
                                                xn[k][:, c, kt * P:(kt + 1) * P], ident[:])
                    last.then_inc(tr_done, 1)
                if live(n):
                    if isinstance(s, int) and s == 1:
                        pe.wait_ge(w_lo, 1)
                    pe.wait_ge(xlo_done, n + 1)
                    cols = bass.ds(n * SEQ, SEQ)
                    for b in range(2):
                        at_least(pe, v_evac, 2 * n + b - 1)
                        for ct in (2 * b, 2 * b + 1):
                            out = ps_v[b][:, (ct % 2) * SEQ:(ct % 2 + 1) * SEQ]
                            ch = slice(ct * P, (ct + 1) * P)
                            for kt in range(KT):
                                last = three_passes(pe, out, w_h[:, kt, ch], w_l[:, kt, ch],
                                                    xh[:, kt, cols], xl[:, kt, cols],
                                                    kt == 0, kt == KT - 1)
                        last.then_inc(v_done, 1)
                    at_least(pe, dt_evac, n)
                    for kt in range(KT):
                        last = three_passes(pe, ps_dt[:, 0:SEQ], w_h[:, kt, DI:], w_l[:, kt, DI:],
                                            xh[:, kt, cols], xl[:, kt, cols], kt == 0, kt == KT - 1)
                    last.then_inc(dt_done, 1)
                if live(m):
                    pe.wait_ge(silu_done, m + 1)
                    for c, evac in ((0, vtok_c0), (1, vtok_c1)):
                        at_least(pe, evac, m)
                        for ct in range(CT):
                            last = pe.transpose(ps_o[c][:, ct * P:(ct + 1) * P],
                                                vs[k][:, ct, c * P:(c + 1) * P], ident[:])
                        last.then_inc(vt_done, 1)
            slots(pe, slot)

        @block.scalar
        def _(act):
            act.wait_ge(w_in, 32)
            act.wait_ge(pad_ready, 3)
            act.activation(w_h[:], w_raw[:], ACT.Copy).then_inc(w_hi, 1)
            act.wait_ge(small_in, 64)

            def slot(s, k):
                n, m = s - 1, s - 2
                if starts(s):
                    act.wait_ge(tr_done, s + 1)
                    act.activation(xh[:, :, bass.ds(s * SEQ, SEQ)],
                                   ps_t[k][:].rearrange("p (a b) -> p a b", a=KT), ACT.Copy
                                   ).then_inc(xhi_done, 1)
                if live(m):
                    act.wait_ge(conv_step, STEPS * (m + 1))
                    at_least(act, vT_out[k], 8 * (m - k))
                    at_least(act, vt_done, 2 * (m - 1))
                    act.activation(vs[k][:], acc[k][:], ACT.Silu).then_inc(silu_done, 1)
                if live(n):
                    j = 1 - k
                    at_least(act, conv_step, STEPS * (n - 1))
                    at_least(act, silu_done, n - 1)
                    for b in range(2):
                        act.wait_ge(v_done, 2 * n + b + 1)
                        act.activation(vbuf[j][:, 2 * b:2 * b + 2, TAPS - 1:],
                                       ps_v[b][:].rearrange("p (a b) -> p a b", a=2), ACT.Copy)
                        for ct in (2 * b, 2 * b + 1):
                            last = act.activation(acc[j][:, ct, :], ps_v[b][:, (ct % 2) * SEQ:(ct % 2 + 1) * SEQ],
                                                  ACT.Identity, bias=conv_b[:, ct:ct + 1],
                                                  scale=taps[:, ct, TAPS - 1:TAPS])
                        last.then_inc(v_evac, 1)
                    act.wait_ge(dt_done, n + 1)
                    act.activation(dt_raw[:, bass.ds(n * SEQ, SEQ)], ps_dt[0:H, 0:SEQ], ACT.Identity,
                                   bias=dt_bias[:, 0:1]).then_inc(dt_evac, 1)
                if live(m):
                    act.wait_ge(vt_done, 2 * m + 1)
                    at_least(act, vtok_out[k], 16 * (m - k))
                    act.activation(vtok[k][:, 0, :], ps_o[0][:], ACT.Copy).then_inc(vtok_c0, 1)
            slots(act, slot)

        @block.vector
        def _(v):
            v.wait_ge(w_hi, 1)
            v.tensor_tensor(w_l[:], w_raw[:], f32(w_h[:]), ALU.subtract).then_inc(w_lo, 1)
            v.wait_ge(small_in, 64)

            def normalise(s, k):
                at_least(v, tr_done, s - 1)
                for c in range(CPS):
                    t = s * CPS + c
                    last = v.tensor_scalar(xn[k][:, c, :], x_sb[:, bass.ds(t, 1), :], mean[:, bass.ds(t, 1)],
                                           rstd[:, bass.ds(t, 1)], ALU.subtract, ALU.mult)
                last.then_inc(xn_ready, 1)

            def slot(s, k):
                n, m = s - 1, s - 2
                if starts(s):
                    v.wait_ge(xhi_done, s + 1)
                    cols = bass.ds(s * SEQ, SEQ)
                    v.tensor_tensor(xl[:, :, cols], ps_t[k][:].rearrange("p (a b) -> p a b", a=KT),
                                    f32(xh[:, :, cols]), ALU.subtract).then_inc(xlo_done, 1)
                if starts(s + 1):
                    normalise(s + 1, 1 - k)
                if live(n):
                    j = 1 - k
                    v.wait_ge(v_evac, 2 * n + 2)
                    for tap in range(TAPS - 1):
                        for ct in range(CT):
                            if tap:
                                v.wait_ge(conv_step, STEPS * n + CT * (tap - 1) + ct + 1)
                            v.scalar_tensor_tensor(acc[j][:, ct, :], vbuf[j][:, ct, tap:tap + SEQ],
                                                   taps[:, ct, tap:tap + 1], acc[j][:, ct, :],
                                                   ALU.mult, ALU.add).then_inc(conv_step, 1)
                if live(m):
                    v.wait_ge(vt_done, 2 * m + 2)
                    at_least(v, vtok_out[k], 16 * (m - k))
                    v.tensor_copy(vtok[k][:, 1, :], ps_o[1][:]).then_inc(vtok_c1, 1)
            normalise(0, 0)
            slots(v, slot)


def stage_decay(nc, d, keep):
    with ExitStack() as ctx:
        sc = Scope(nc, ctx, "dec")
        dt, cumT = keep["dt"], keep["cumT"]
        az, ex, cum, carry = (sc.sb(n, [H, TOK]) for n in ("az", "ex", "cum", "carry"))
        a_log, na, ident = sc.sb("a_log", [H, 1]), sc.sb("na", [H, 1]), sc.sb("ident", [H, H])
        ps = [sc.bank(f"ps{b}") for b in range(2)]
        small_in, ones, carry_ready, a_exp, na_done = (
            sc.sem(n) for n in ("small_in", "ones", "carry_ready", "a_exp", "na_done"))
        az_done, ex_done, ln_done, sp_done, ld_done, cum_done, tr_done, cumT_done, cum_out = (
            sc.sem(n) for n in ("az_done", "ex_done", "ln_done", "sp_done", "ld_done", "cum_done",
                                "tr_done", "cumT_done", "cum_out"))
        CH = 4
        W = TOK // CH
        part = [slice(c * W, (c + 1) * W) for c in range(CH)]
        block = ctx.enter_context(nc.Block())

        @block.sync
        def _(sp):
            sp.dma_start(a_log[:], d["a_log"]).then_inc(small_in, 16)
            sp.dma_start(ident[:], d["ident"][0:H, 0:H]).then_inc(small_in, 16)
            for c in range(CH):
                sp.wait_ge(cum_done, c + 1)
                sp.dma_start(d["cum"][:, part[c]], cum[:, part[c]]).then_inc(cum_out, 16)
            sp.wait_ge(cum_out, 16 * CH)

        @block.gpsimd
        def _(pool):
            pool.memset(carry[:], 1.0).then_inc(ones, 1)
            pool.wait_ge(ones, 1)
            pool.memset(carry[:].rearrange("h (s l) -> h s l", l=SEQ)[:, :, 0:1], 0.0).then_inc(carry_ready, 1)

        @block.scalar
        def _(act):
            act.wait_ge(small_in, 32)
            act.activation(na[:], a_log[:], ACT.Exp).then_inc(a_exp, 1)
            for c in range(CH):
                act.wait_ge(az_done, c + 1)
                act.activation(ex[:, part[c]], az[:, part[c]], ACT.Exp).then_inc(ex_done, 1)
            for c in range(CH):
                act.wait_ge(ex_done, c + 1)
                act.activation(ex[:, part[c]], ex[:, part[c]], ACT.Ln, bias=1.0).then_inc(ln_done, 1)

        @block.vector
        def _(v):
            for c in range(CH):
                v.scalar_tensor_tensor(az[:, part[c]], dt[:, part[c]], -1.0, dt[:, part[c]],
                                       ALU.mult, ALU.min).then_inc(az_done, 1)
            v.wait_ge(a_exp, 1)
            v.tensor_scalar(na[:], na[:], -1.0, None, ALU.mult).then_inc(na_done, 1)
            v.wait_ge(na_done, 1)
            v.wait_ge(carry_ready, 1)
            for c in range(CH):
                v.wait_ge(ln_done, c + 1)
                v.scalar_tensor_tensor(dt[:, part[c]], dt[:, part[c]], 0.0, ex[:, part[c]],
                                       ALU.max, ALU.add).then_inc(sp_done, 1)
                v.wait_ge(sp_done, c + 1)
                v.tensor_scalar(dt[:, part[c]], dt[:, part[c]], na[:, 0:1], None, ALU.mult).then_inc(ld_done, 1)
                v.wait_ge(ld_done, c + 1)
                v.tensor_tensor_scan(cum[:, part[c]], carry[:, part[c]], dt[:, part[c]], 0.0,
                                     ALU.mult, ALU.add).then_inc(cum_done, 1)
            for b in range(2):
                v.wait_ge(tr_done, b + 1)
                v.tensor_copy(cumT[:, b * 16:(b + 1) * 16, :],
                              ps[b][:].rearrange("p (t h) -> p t h", h=H)).then_inc(cumT_done, 1)

        @block.tensor
        def _(pe):
            pe.wait_ge(small_in, 32)
            for b in range(2):
                for t in range(16):
                    tile = b * 16 + t
                    if tile % 8 == 0:
                        pe.wait_ge(cum_done, tile // 8 + 1)
                    last = pe.transpose(ps[b][:, t * H:(t + 1) * H], cum[:, tile * P:(tile + 1) * P], ident[:])
                last.then_inc(tr_done, 1)


def stage_mixer(nc, d, keep):
    with ExitStack() as ctx:
        sc = Scope(nc, ctx, "mix")
        xh, xl, cumT = (keep[n] for n in ("xh", "xl", "cumT"))
        mask = sc.sb("mask", [P, P])
        w_raw = [sc.sb(f"w_raw{j}", [P, KT, 2 * N]) for j in range(GH)]
        w_h = [sc.sb(f"w_h{j}", [P, KT, 2 * N], F32R) for j in range(GH)]
        w_l = [sc.sb(f"w_l{j}", [P, KT, 2 * N], F32R) for j in range(GH)]
        cum = [sc.sb(f"cum{k}", [P, GH, SEQ]) for k in range(2)]
        vst = [sc.sb(f"vst{k}", [P, CPS, GCH]) for k in range(2)]
        vp = [sc.sb(f"vp{k}", [P, CPS, GH, 2, GCH], F32R) for k in range(2)]
        d_param = sc.sb("d_param", [GCH, GROUPS])
        vT = [sc.sb(f"vT{k}", [GCH, SEQ]) for k in range(2)]
        dv = [sc.sb(f"dv{k}", [GCH, SEQ]) for k in range(2)]
        y_lo = sc.sb("y_lo", [GCH, SEQ])
        LW = SEQ + P
        dec = [sc.sb(f"dec{k}", [P, GH, LW]) for k in range(2)]
        bc_h = [sc.sb(f"bc_h{k}", [P, 2 * SEQ], F32R) for k in range(2)]
        bc_l = [sc.sb(f"bc_l{k}", [P, 2 * SEQ], F32R) for k in range(2)]
        m_f = [sc.sb(f"m_f{k}", [P, LW]) for k in range(2)]
        m_h = [sc.sb(f"m_h{k}", [P, LW], F32R) for k in range(4)]
        m_l = [sc.sb(f"m_l{k}", [P, LW], F32R) for k in range(4)]
        yst = [sc.sb(f"yst{k}", [GCH, SEQ]) for k in range(2)]
        ps_p = [sc.bank(f"ps_p{k}") for k in range(4)]
        ps_c = [sc.bank(f"ps_c{k}") for k in range(2)]
        ps_y = [sc.bank(f"ps_y{k}") for k in range(2)]
        small_in, zeroed = sc.sem("small_in"), sc.sem("zeroed")
        vT_in = [sc.sem(f"vT_in{k}") for k in range(2)]
        dv_done, ylo_done, yhi_done = sc.sem("dv_done"), sc.sem("ylo_done"), sc.sem("yhi_done")
        w_in = [sc.sem(f"w_in{j}") for j in range(GH)]
        cum_in = [sc.sem(f"cum_in{k}") for k in range(2)]
        v_in = [sc.sem(f"v_in{k}") for k in range(2)]
        y_out = [sc.sem(f"y_out{k}") for k in range(2)]
        w_hi, w_lo = sc.sem("w_hi"), sc.sem("w_lo")
        dif_done, msk_done, vh_done, vp_done = (
            sc.sem(n) for n in ("dif_done", "msk_done", "vh_done", "vp_done"))
        p_done, bh_done, bl_done, c_done, exp_done = (
            sc.sem(n) for n in ("p_done", "bh_done", "bl_done", "c_done", "exp_done"))
        mt_done, mh_done, ml_done, pv_done, y_evac = (
            sc.sem(n) for n in ("mt_done", "mh_done", "ml_done", "pv_done", "y_evac"))
        ITERS = GROUPS * SEQS
        UNITS = GH * ITERS
        block = ctx.enter_context(nc.Block())

        def walk(eng, iteration, new_group=None, after_first=None):
            if new_group:
                new_group(0)
            for i in range(4):
                if after_first and i == 2:
                    after_first(0)
                iteration(i, 0, i, i % 2)
            with eng.Fori(2, SEQS // 2) as q:
                for k in range(2):
                    iteration(q * 2 + k, 0, q * 2 + k, k)
            with eng.Fori(1, GROUPS) as g:
                if new_group:
                    new_group(g)
                if after_first:
                    for k in range(2):
                        iteration(g * SEQS + k, g, k, k)
                    after_first(g)
                with eng.Fori(1 if after_first else 0, SEQS // 2) as q:
                    for k in range(2):
                        s = q * 2 + k
                        iteration(g * SEQS + s, g, s, k)
            for i in range(ITERS, ITERS + 4):
                iteration(i, GROUPS - 1, i, i % 2)

        def live(n, end):
            return not isinstance(n, int) or 0 <= n < end

        @block.sync
        def _(sp):
            sp.dma_start(mask[:], d["mask"]).then_inc(small_in, 16)
            sp.dma_start(d_param[:], d["d_param"]).then_inc(small_in, 16)

            def load_weights(g):
                for j in range(GH):
                    at_least(sp, w_lo, g * GH + j - GH + 1)
                    sp.dma_start(w_raw[j][:], d["w_bc"][bass.ds((g % GROUPS) * GH + j, 1)].rearrange("h p k n -> p (h k) n")
                                 ).then_inc(w_in[j], 16)

            def iteration(i, g, s, k):
                if live(i, ITERS):
                    at_least(sp, msk_done, i - 1)
                    sp.dma_start(cum[k][:], d["cum"][bass.ds(g * GH, GH), bass.ds(s * SEQ, SEQ)]
                                 .partition_broadcast(P)).then_inc(cum_in[k], 16)
                    at_least(sp, vp_done, i - 1)
                    sp.dma_start(vst[k][:], d["val"][bass.ds(s, 1), bass.ds(g, 1)]
                                 .rearrange("s g p c q -> p (s g c) q")).then_inc(v_in[k], 16)
                    at_least(sp, dv_done, i - 1)
                    sp.dma_start(vT[k][:], d["vT"][bass.ds(g * GCH, GCH), bass.ds(s * SEQ, SEQ)]
                                 ).then_inc(vT_in[k], 16)
                if live(i - 3, ITERS):
                    sp.wait_ge(y_evac, i - 2)
                    sp.dma_start(d["y"][bass.ds(i - 3, 1)].rearrange("i c l -> (i c) l"), yst[1 - k][:]
                                 ).then_inc(y_out[1 - k], 16)

            def next_weights(g):
                load_weights(g + 1)

            load_weights(0)
            walk(sp, iteration, None, next_weights)
            for k in range(2):
                sp.wait_ge(y_out[k], 16 * (ITERS // 2))
            for j in range(GH):
                sp.wait_ge(w_in[j], 16 * (GROUPS + 1))

        @block.gpsimd
        def _(pool):
            for k in range(2):
                pool.memset(f32(vp[k][:]), 0.0).then_inc(zeroed, 1)
            pool.wait_ge(zeroed, 2)
            pool.wait_ge(small_in, 32)

            def diag(k, part):
                return bass.AP(vp[k], part * GCH, [[CPS * GH * P, P], [GH * P, CPS], [P + HD, GH], [1, HD]])

            def iteration(i, g, s, k):
                if live(i, ITERS):
                    pool.wait_ge(cum_in[k], 8 * (i - k) + 16)
                    at_least(pool, mt_done, GH * (i - 1))
                    for c in range(CPS):
                        row = cumT[:, bass.ds(s * CPS + c, 1), bass.ds(g * GH, GH)].rearrange("p o h -> p (o h)")
                        w = SEQ if c == 0 else P
                        pool.tensor_tensor(dec[k][:, :, c * SEQ:c * SEQ + w], cum[k][:, :, c * P:c * P + w],
                                           row.unsqueeze(2).broadcast_to([P, GH, w]), ALU.subtract
                                           ).then_inc(dif_done, 1)
                    pool.wait_ge(dif_done, 2 * i + 2)
                    pool.wait_ge(v_in[k], 8 * (i - k) + 16)
                    at_least(pool, pv_done, GH * (i - 1))
                    tri = dec[k][:].rearrange("p h (b l) -> p h b l", l=P)[:, :, 0:3:2, :]
                    pool.tensor_tensor(tri, tri, mask[:].unsqueeze(1).unsqueeze(1).broadcast_to([P, GH, 2, P]),
                                       ALU.add).then_inc(msk_done, 1)
                    v4 = vst[k][:].rearrange("p c (h q) -> p c h q", q=HD)
                    pool.tensor_copy(diag(k, 0), v4).then_inc(vh_done, 1)
                    pool.wait_ge(vh_done, i + 1)
                    pool.tensor_tensor(diag(k, 1), v4, diag(k, 0).bitcast(F32), ALU.subtract
                                       ).then_inc(vp_done, 1)
            walk(pool, iteration)

        @block.tensor
        def _(pe):
            pe.wait_ge(zeroed, 2)

            def iteration(i, g, s, k):
                cols = None
                for j in range(GH):
                    t = i * GH + j
                    if live(i, ITERS):
                        pe.wait_ge(w_lo, g * GH + j + 1)
                        at_least(pe, bl_done, t - 3)
                        cols = bass.ds(s * SEQ, SEQ)
                        for b in range(2):
                            for kt in range(KT):
                                last = three_passes(
                                    pe, ps_p[j][:, b * SEQ:(b + 1) * SEQ],
                                    w_h[j][:, kt, b * N:(b + 1) * N], w_l[j][:, kt, b * N:(b + 1) * N],
                                    xh[:, kt, cols], xl[:, kt, cols], kt == 0, kt == KT - 1)
                        last.then_inc(p_done, 1)
                    if live(t - 2, UNITS):
                        pe.wait_ge(bl_done, t - 1)
                        at_least(pe, mt_done, t - 3)
                        b_h, b_l = bc_h[j % 2], bc_l[j % 2]
                        for c in range(CPS):
                            m = slice(c * P, (c + 1) * P)
                            l = slice(SEQ + c * P, 2 * SEQ)
                            last = three_passes(pe, ps_c[j % 2][:, c * SEQ:c * SEQ + SEQ - c * P],
                                                b_h[:, m], b_l[:, m], b_h[:, l], b_l[:, l], True, True)
                        last.then_inc(c_done, 1)
                    if live(t - 4, UNITS):
                        n, o = i - 1, 1 - k
                        if j == 0:
                            pe.wait_ge(vp_done, n + 1)
                            at_least(pe, y_evac, n - 1)
                        pe.wait_ge(ml_done, t - 3)
                        for c in range(CPS):
                            seen = slice(c * P, SEQ)
                            mine = slice(c * SEQ, c * SEQ + SEQ - c * P)
                            pe.matmul(ps_y[o][:, seen], vp[o][:, c, j, :, :].rearrange("p h q -> p (h q)"),
                                      m_h[j][:, mine], start=(j == 0 and c == 0), stop=False,
                                      skip_group_check=True)
                            last = pe.matmul(ps_y[o][0:GCH, seen], vp[o][:, c, j, 0, :], m_l[j][:, mine],
                                             start=False, stop=(j == GH - 1 and c == CPS - 1),
                                             skip_group_check=True)
                        last.then_inc(pv_done, 1)
            walk(pe, iteration)

        @block.scalar
        def _(act):
            act.wait_ge(small_in, 32)

            def new_group(g):
                for j in range(GH):
                    act.wait_ge(w_in[j], g * 16 + 16)
                    at_least(act, p_done, g * (GH * SEQS) - GH + j + 1)
                    act.activation(w_h[j][:], w_raw[j][:], ACT.Copy).then_inc(w_hi, 1)

            def iteration(i, g, s, k):
                if live(i - 2, ITERS):
                    act.wait_ge(pv_done, GH * (i - 1))
                    at_least(act, y_evac, i - 2)
                    act.activation(y_lo[:], ps_y[k][GCH:, 0:SEQ], ACT.Copy).then_inc(ylo_done, 1)
                for j in range(GH):
                    t = i * GH + j
                    if live(t - 3, UNITS):
                        r = (j + 1) % 4
                        act.wait_ge(mt_done, t - 2)
                        at_least(act, pv_done, t - 6)
                        act.activation(m_h[r][:], m_f[(j + 1) % 2][:], ACT.Copy).then_inc(mh_done, 1)
                    if live(i, ITERS):
                        act.wait_ge(p_done, t + 1)
                        at_least(act, c_done, t - 1)
                        if j == 3:
                            act.wait_ge(vT_in[k], 8 * (i - k) + 16)
                            at_least(act, yhi_done, i - 1)
                        act.activation(bc_h[j % 2][:], ps_p[j][:], ACT.Copy).then_inc(bh_done, 1)
                        if j < 2:
                            act.wait_ge(msk_done, i + 1)
                            half = dec[k][:, 2 * j:2 * j + 2, :]
                            act.activation(half, half, ACT.Exp).then_inc(exp_done, 1)
                        if j == 3:
                            act.activation(dv[k][:], vT[k][:], ACT.Copy, scale=d_param[:, bass.ds(g, 1)]
                                           ).then_inc(dv_done, 1)
            walk(act, iteration, new_group)

        @block.vector
        def _(v):
            def new_group(g):
                for j in range(GH):
                    v.wait_ge(w_hi, g * GH + j + 1)
                    v.tensor_tensor(w_l[j][:], w_raw[j][:], f32(w_h[j][:]), ALU.subtract).then_inc(w_lo, 1)

            def iteration(i, g, s, k):
                for j in range(GH):
                    t = i * GH + j
                    if j == 1 and live(i - 2, ITERS):
                        v.wait_ge(pv_done, GH * (i - 1))
                        v.wait_ge(dv_done, i - 1)
                        at_least(v, y_out[k], 8 * (i - k) - 16)
                        v.tensor_tensor(yst[k][:], ps_y[k][0:GCH, 0:SEQ], dv[k][:], ALU.add).then_inc(yhi_done, 1)
                    if j == 2 and live(i - 2, ITERS):
                        v.wait_ge(ylo_done, i - 1)
                        v.wait_ge(yhi_done, i - 1)
                        v.tensor_tensor(yst[k][:], yst[k][:], y_lo[:], ALU.add).then_inc(y_evac, 1)
                    if live(t - 3, UNITS):
                        r = (j + 1) % 4
                        v.wait_ge(mh_done, t - 2)
                        at_least(v, pv_done, t - 6)
                        v.tensor_tensor(m_l[r][:], m_f[(j + 1) % 2][:], f32(m_h[r][:]), ALU.subtract
                                        ).then_inc(ml_done, 1)
                    if live(t - 2, UNITS):
                        r = (j + 2) % 4
                        kk = k if j >= 2 else 1 - k
                        n = i if j >= 2 else i - 1
                        v.wait_ge(c_done, t - 1)
                        v.wait_ge(exp_done, n * 2 + r // 2 + 1)
                        v.tensor_tensor(m_f[j % 2][:], ps_c[j % 2][:, 0:LW], dec[kk][:, r, :], ALU.mult
                                        ).then_inc(mt_done, 1)
                    if live(i, ITERS):
                        v.wait_ge(bh_done, t + 1)
                        v.tensor_tensor(bc_l[j % 2][:], ps_p[j][:], f32(bc_h[j % 2][:]), ALU.subtract
                                        ).then_inc(bl_done, 1)
            walk(v, iteration, new_group)


def split_on_chip(nc, name, items):
    with ExitStack() as ctx:
        sc = Scope(nc, ctx, name)
        raws = [sc.sb(f"raw_{label}", list(hi.shape)) for label, hi, _, _ in items]
        loaded = [sc.sem(f"loaded_{label}") for label, _, _, _ in items]
        zeroed, hi_done, lo_done = sc.sem("zeroed"), sc.sem("hi_done"), sc.sem("lo_done")
        block = ctx.enter_context(nc.Block())

        @block.gpsimd
        def _(pool):
            for raw in raws:
                pool.memset(raw[:], 0.0).then_inc(zeroed, 1)

        @block.sync
        def _(sp):
            for i, (_, _, _, loads) in enumerate(items):
                sp.wait_ge(zeroed, i + 1)
                for where, src in loads:
                    sp.dma_start(raws[i][where], src).then_inc(loaded[i], 16)

        @block.scalar
        def _(act):
            for i, (_, hi, _, loads) in enumerate(items):
                act.wait_ge(loaded[i], 16 * len(loads))
                act.activation(hi[:], raws[i][:], ACT.Copy).then_inc(hi_done, 1)

        @block.vector
        def _(v):
            for i, (_, hi, lo, _) in enumerate(items):
                v.wait_ge(hi_done, i + 1)
                v.tensor_tensor(lo[:], raws[i][:], f32(hi[:]), ALU.subtract).then_inc(lo_done, 1)


def stage_mixer_out(nc, d, keep):
    with ExitStack() as ctx:
        sc = Scope(nc, ctx, "out")
        x_sb, mean, rstd, xh, xl = (keep[n] for n in ("x", "mean", "rstd", "xh", "xl"))
        wg_h, wg_l = (sc.sb(n, [P, KT, DI], F32R) for n in ("wg_h", "wg_l"))
        wo_h, wo_l = (sc.sb(n, [P, CT, DM], F32R) for n in ("wo_h", "wo_l"))
        every = (slice(None), slice(None), slice(None))
        split_on_chip(nc, "outw", [("gate", wg_h, wg_l, [(every, d["w_gate"])]),
                                   ("out", wo_h, wo_l, [(every, d["w_out"])])])
        st = sc.sb("st", [P, TILES, 6])
        yb = [sc.sb(f"yb{k}", [P, CT, BLK]) for k in range(2)]
        sg = [sc.sb(f"sg{ct}", [P, BLK]) for ct in range(CT)]
        u_h = [sc.sb(f"u_h{k}", [P, CT, BLK], F32R) for k in range(2)]
        u_l = [sc.sb(f"u_l{k}", [P, CT, BLK], F32R) for k in range(2)]
        ps_g = [sc.bank(f"ps_g{ct}") for ct in range(CT)]
        ps_o = [sc.bank(f"ps_o{b}") for b in range(2)]
        y_in = [sc.sem(f"y_in{k}") for k in range(2)]
        g_done, sg_done, u_done, uh_done, ul_done = (
            sc.sem(n) for n in ("g_done", "sg_done", "u_done", "uh_done", "ul_done"))
        o_done, x_done, stats_done, step, var_ready, root_done, rstd_done, x_out = (
            sc.sem(n) for n in ("o_done", "x_done", "stats_done", "step", "var_ready", "root_done",
                                "rstd_done", "x_out"))
        block = ctx.enter_context(nc.Block())

        def slots(eng, slot):
            for n in range(2):
                slot(n, n % 2)
            with eng.Fori(1, NBLK // 2) as q:
                for k in range(2):
                    slot(q * 2 + k, k)
            for n in range(NBLK, NBLK + 2):
                slot(n, n % 2)

        def live(n):
            return not isinstance(n, int) or 0 <= n < NBLK

        @block.sync
        def _(sp):
            y_view = d["y"].rearrange("(c f s) r l -> f r c s l", c=CT, f=2)

            def slot(n, k):
                if live(n):
                    at_least(sp, ul_done, CT * (n - 1))
                    for half in range(2):
                        rows = slice(half * GCH, (half + 1) * GCH)
                        for ct in range(CT):
                            sp.dma_start(yb[k][rows, ct, :].rearrange("p (s l) -> p s l", l=SEQ),
                                         y_view[half, :, ct, bass.ds(n * 2, 2), :]).then_inc(y_in[k], 16)
                if live(n - 2):
                    sp.wait_ge(x_done, 2 * (n - 1))
                    sp.dma_start(d["x1"][:, bass.ds((n - 2) * TPB, TPB), :],
                                 x_sb[:, bass.ds((n - 2) * TPB, TPB), :]).then_inc(x_out, 16)
            slots(sp, slot)
            sp.wait_ge(x_out, 16 * NBLK)

        @block.tensor
        def _(pe):
            def slot(n, k):
                m = n - 1
                if live(n):
                    for ct in range(CT):
                        at_least(pe, sg_done, CT * (n - 1) + ct + 1)
                        for kt in range(KT):
                            last = three_passes(pe, ps_g[ct][:], wg_h[:, kt, ct * P:(ct + 1) * P],
                                                wg_l[:, kt, ct * P:(ct + 1) * P],
                                                xh[:, kt, bass.ds(n * BLK, BLK)], xl[:, kt, bass.ds(n * BLK, BLK)],
                                                kt == 0, kt == KT - 1)
                        last.then_inc(g_done, 1)
                if live(m):
                    pe.wait_ge(ul_done, CT * n)
                    for b in range(2):
                        at_least(pe, x_done, 2 * (m - 1) + b + 1)
                        for q in (2 * b, 2 * b + 1):
                            tok = slice(q * P, (q + 1) * P)
                            for ct in range(CT):
                                last = three_passes(pe, ps_o[b][:, (q % 2) * DM:(q % 2 + 1) * DM],
                                                    u_h[1 - k][:, ct, tok], u_l[1 - k][:, ct, tok],
                                                    wo_h[:, ct, :], wo_l[:, ct, :], ct == 0, ct == CT - 1)
                        last.then_inc(o_done, 1)
            slots(pe, slot)

        @block.scalar
        def _(act):
            def slot(n, k):
                if live(n):
                    for ct in range(CT):
                        act.wait_ge(g_done, CT * n + ct + 1)
                        at_least(act, u_done, CT * (n - 1) + ct + 1)
                        act.activation(sg[ct][:], ps_g[ct][:], ACT.Silu).then_inc(sg_done, 1)
                    for ct in range(CT):
                        act.wait_ge(u_done, CT * n + ct + 1)
                        at_least(act, o_done, 2 * (n - 1))
                        act.activation(u_h[k][:, ct, :], yb[k][:, ct, :], ACT.Copy).then_inc(uh_done, 1)
            slots(act, slot)
            act.wait_ge(var_ready, 1)
            act.activation(rstd[:], rstd[:], ACT.Sqrt).then_inc(root_done, 1)

        @block.gpsimd
        def _(pool):
            def slot(n, k):
                if live(n):
                    pool.wait_ge(y_in[k], 64 * (n - k) + 128)
                    for ct in range(CT):
                        pool.wait_ge(sg_done, CT * n + ct + 1)
                        pool.tensor_tensor(yb[k][:, ct, :], yb[k][:, ct, :], sg[ct][:], ALU.mult
                                           ).then_inc(u_done, 1)
            slots(pool, slot)

        @block.vector
        def _(v):
            def slot(n, k):
                m = n - 1
                if live(n):
                    for ct in range(CT):
                        v.wait_ge(uh_done, CT * n + ct + 1)
                        v.tensor_tensor(u_l[k][:, ct, :], yb[k][:, ct, :], f32(u_h[k][:, ct, :]), ALU.subtract
                                        ).then_inc(ul_done, 1)
                if live(m):
                    for b in range(2):
                        v.wait_ge(o_done, 2 * m + b + 1)
                        two = bass.ds(m * TPB + 2 * b, 2)
                        v.tensor_tensor(x_sb[:, two, :], ps_o[b][:].rearrange("p (q d) -> p q d", q=2),
                                        x_sb[:, two, :], ALU.add).then_inc(x_done, 1)
                    for q in range(TPB):
                        v.wait_ge(x_done, 2 * m + q // 2 + 1)
                        one = bass.ds(m * TPB + q, 1)
                        v.bn_stats(st[:, one, :].rearrange("p o s -> p (o s)"),
                                   x_sb[:, one, :].rearrange("p o d -> p (o d)")).then_inc(stats_done, 1)
            slots(v, slot)
            finish_moments(v, st, mean, rstd, stats_done, step, var_ready, root_done, rstd_done)


def stage_route(nc, d, keep):
    with ExitStack() as ctx:
        sc = Scope(nc, ctx, "rt")
        x_sb, mean, rstd = keep["x"], keep["mean"], keep["rstd"]
        wr_h, wr_l = (sc.sb(n, [P, KT, P], F32R) for n in ("wr_h", "wr_l"))
        split_on_chip(nc, "rtw", [("route", wr_h, wr_l, [((slice(None), slice(None), slice(0, E)), d["w_route"])])])
        ident = sc.sb("ident", [P, P])
        rank = sc.sb("rank", [P, E])
        xn = [sc.sb(f"xn{k}", [P, TPB, DM]) for k in range(2)]
        x2h = [sc.sb(f"x2h{k}", [P, KT, BLK], F32R) for k in range(2)]
        x2l = [sc.sb(f"x2l{k}", [P, KT, BLK], F32R) for k in range(2)]
        lgT = [sc.sb(f"lgT{k}", [P, BLK]) for k in range(2)]
        lg = sc.sb("lg", [P, TILES, E])
        cand = sc.sb("cand", [P, TILES, E])
        best = sc.sb("best", [P, TILES])
        top = sc.sb("top", [P, CPS, 2, SEQS])
        hot = sc.sb("hot", [P, TILES, 2, E])
        hotT = sc.sb("hotT", [P, 4, P])
        mx, tot, inv = (sc.sb(n, [2 * SEQS, 1]) for n in ("mx", "tot", "inv"))
        soft = sc.sb("soft", [2 * SEQS, SEQ])
        ps_t = [[sc.bank(f"ps_t{k}{kt}") for kt in range(KT)] for k in range(2)]
        ps_l = sc.bank("ps_l")
        ps_lt = sc.bank("ps_lt")
        ps_top, ps_hot = sc.bank("ps_top"), sc.bank("ps_hot")
        small_in = sc.sem("small_in")
        xn_ready, tr_done, hi_done, lo_done, l_done, lT_done, lt_done, lg_done = (
            sc.sem(n) for n in ("xn_ready", "tr_done", "hi_done", "lo_done", "l_done", "lT_done",
                                "lt_done", "lg_done"))
        x2_out = [sc.sem(f"x2_out{k}") for k in range(2)]
        step, top_done, topT_done, mx_done, soft_exp, soft_done, hotT_done, hot_copied, out = (
            sc.sem(n) for n in ("step", "top_done", "topT_done", "mx_done", "soft_exp", "soft_done",
                                "hotT_done", "hot_copied", "out"))
        block = ctx.enter_context(nc.Block())

        def slots(eng, slot):
            for n in range(2):
                slot(n, n % 2)
            with eng.Fori(1, NBLK // 2) as q:
                for k in range(2):
                    slot(q * 2 + k, k)
            for n in range(NBLK, NBLK + 2):
                slot(n, n % 2)

        def live(n):
            return not isinstance(n, int) or 0 <= n < NBLK

        @block.sync
        def _(sp):
            sp.dma_start(ident[:], d["ident"]).then_inc(small_in, 16)
            sp.dma_start(rank[:], d["rank"]).then_inc(small_in, 16)

            def slot(n, k):
                if live(n):
                    sp.wait_ge(hi_done, n + 1)
                    sp.dma_start(d["x2h"][bass.ds(n, 1)].rearrange("n p k l -> p (n k) l"), f32(x2h[k][:])
                                 ).then_inc(x2_out[k], 16)
                    sp.wait_ge(lo_done, n + 1)
                    sp.dma_start(d["x2l"][bass.ds(n, 1)].rearrange("n p k l -> p (n k) l"), f32(x2l[k][:])
                                 ).then_inc(x2_out[k], 16)
            slots(sp, slot)
            sp.wait_ge(hot_copied, 1)
            for b in range(4):
                for t in range(8):
                    sp.dma_start(d["hot"][:, (b * 8 + t) * P:(b * 8 + t + 1) * P],
                                 hotT[t * 2 * E:(t + 1) * 2 * E, b, :]).then_inc(out, 16)
            sp.wait_ge(soft_done, 1)
            sp.dma_start(d["soft"].rearrange("r (s l) -> (r s) l", l=SEQ), soft[:]).then_inc(out, 16)
            sp.wait_ge(out, 33 * 16)
            for k in range(2):
                sp.wait_ge(x2_out[k], 32 * (NBLK // 2))

        @block.tensor
        def _(pe):
            pe.wait_ge(small_in, 32)

            def slot(n, k):
                m, o = n - 1, n - 2
                if live(n):
                    pe.wait_ge(xn_ready, n + 1)
                    at_least(pe, lo_done, n - 1)
                    for kt in range(KT):
                        for q in range(TPB):
                            last = pe.transpose(ps_t[k][kt][:, q * P:(q + 1) * P],
                                                xn[k][:, q, kt * P:(kt + 1) * P], ident[:])
                    last.then_inc(tr_done, 1)
                if live(m):
                    pe.wait_ge(lo_done, m + 1)
                    at_least(pe, lT_done, m)
                    for kt in range(KT):
                        last = three_passes(pe, ps_l[:], wr_h[:, kt, :], wr_l[:, kt, :],
                                            x2h[1 - k][:, kt, :], x2l[1 - k][:, kt, :], kt == 0, kt == KT - 1)
                    last.then_inc(l_done, 1)
                if live(o):
                    pe.wait_ge(lT_done, o + 1)
                    at_least(pe, lg_done, o)
                    for q in range(TPB):
                        last = pe.transpose(ps_lt[:, q * P:(q + 1) * P], lgT[k][:, q * P:(q + 1) * P], ident[:])
                    last.then_inc(lt_done, 1)
            slots(pe, slot)
            pe.wait_ge(top_done, 2)
            for c in range(CPS):
                last = pe.transpose(ps_top[0:2 * SEQS, c * P:(c + 1) * P],
                                    top[:, c, :, :].rearrange("p r s -> p (r s)"), ident[:])
            last.then_inc(topT_done, 1)
            pe.wait_ge(step, 11)
            for b in range(4):
                last = pe.transpose(ps_hot[:, b * P:(b + 1) * P],
                                    hot[:, b * 8:(b + 1) * 8, :, :].rearrange("p t r e -> p (t r e)"), ident[:])
            last.then_inc(hotT_done, 1)

        @block.scalar
        def _(act):
            def slot(n, k):
                m = n - 1
                if live(n):
                    act.wait_ge(tr_done, n + 1)
                    at_least(act, x2_out[k], 16 * (n - k))
                    at_least(act, l_done, n - 1)
                    for kt in range(KT):
                        last = act.activation(x2h[k][:, kt, :], ps_t[k][kt][:], ACT.Copy)
                    last.then_inc(hi_done, 1)
                if live(m):
                    act.wait_ge(l_done, m + 1)
                    at_least(act, lt_done, m - 1)
                    act.activation(lgT[1 - k][:], ps_l[:], ACT.Copy).then_inc(lT_done, 1)
            slots(act, slot)
            act.wait_ge(mx_done, 1)
            act.activation(soft[:], ps_top[0:2 * SEQS, 0:SEQ], ACT.Exp, bias=mx[:, 0:1],
                           accum_out=tot[:, 0:1]).then_inc(soft_exp, 1)
            act.wait_ge(hotT_done, 1)
            act.activation(hotT[:].rearrange("p b l -> p (b l)"), ps_hot[:], ACT.Copy).then_inc(hot_copied, 1)

        @block.vector
        def _(v):
            v.wait_ge(small_in, 32)

            def slot(n, k):
                o = n - 2
                if live(n):
                    at_least(v, tr_done, n - 1)
                    for q in range(TPB):
                        t = n * TPB + q
                        last = v.tensor_scalar(xn[k][:, q, :], x_sb[:, bass.ds(t, 1), :], mean[:, bass.ds(t, 1)],
                                               rstd[:, bass.ds(t, 1)], ALU.subtract, ALU.mult)
                    last.then_inc(xn_ready, 1)
                    v.wait_ge(hi_done, n + 1)
                    for kt in range(KT):
                        last = v.tensor_tensor(x2l[k][:, kt, :], ps_t[k][kt][:], f32(x2h[k][:, kt, :]), ALU.subtract)
                    last.then_inc(lo_done, 1)
                if live(o):
                    v.wait_ge(lt_done, o + 1)
                    v.tensor_copy(lg[:, bass.ds(o * TPB, TPB), :],
                                  ps_lt[:].rearrange("p (q e) -> p q e", q=TPB)[:, :, 0:E]).then_inc(lg_done, 1)
            slots(v, slot)
            v.wait_ge(lg_done, NBLK)
            wide = [P, TILES, E]
            steps = 0
            for r in range(2):
                v.tensor_reduce(best[:], lg[:], AX_X, ALU.max).then_inc(step, 1)
                steps += 1
                v.wait_ge(step, steps)
                v.tensor_copy(top[:, :, r, :].rearrange("p c s -> p s c"),
                              best[:].rearrange("p (s c) -> p s c", c=CPS)).then_inc(top_done, 1)
                v.tensor_tensor(cand[:], lg[:], best[:].unsqueeze(2).broadcast_to(wide), ALU.is_equal
                                ).then_inc(step, 1)
                steps += 1
                v.wait_ge(step, steps)
                v.tensor_tensor(cand[:], cand[:], rank[:].unsqueeze(1).broadcast_to(wide), ALU.mult).then_inc(step, 1)
                steps += 1
                v.wait_ge(step, steps)
                v.wait_ge(top_done, r + 1)
                v.tensor_reduce(best[:], cand[:], AX_X, ALU.max).then_inc(step, 1)
                steps += 1
                v.wait_ge(step, steps)
                v.tensor_tensor(hot[:, :, r, :], cand[:], best[:].unsqueeze(2).broadcast_to(wide), ALU.is_equal
                                ).then_inc(step, 1)
                steps += 1
                v.wait_ge(step, steps)
                if r == 0:
                    v.scalar_tensor_tensor(lg[:], hot[:, :, 0, :], -3.0e38, lg[:], ALU.mult, ALU.add
                                           ).then_inc(step, 1)
                    steps += 1
                    v.wait_ge(step, steps)
            v.wait_ge(topT_done, 1)
            v.tensor_reduce(mx[:], ps_top[0:2 * SEQS, 0:SEQ], AX_X, ALU.max).then_inc(step, 1)
            v.wait_ge(step, steps + 1)
            v.tensor_scalar(mx[:], mx[:], -1.0, None, ALU.mult).then_inc(mx_done, 1)
            v.wait_ge(soft_exp, 1)
            v.reciprocal(inv[:], tot[:]).then_inc(step, 1)
            v.wait_ge(step, steps + 2)
            v.tensor_scalar(soft[:], soft[:], inv[:, 0:1], None, ALU.mult).then_inc(soft_done, 1)


def stage_experts(nc, d):
    with ExitStack() as ctx:
        sc = Scope(nc, ctx, "ffn")
        HP = HT * P
        wu_h, wu_l, wg_h, wg_l = (sc.sb(n, [P, KT, HP], F32R) for n in ("wu_h", "wu_l", "wg_h", "wg_l"))
        bu_h, bu_l, bg_h, bg_l = (sc.sb(n, [P, HP], F32R) for n in ("bu_h", "bu_l", "bg_h", "bg_l"))
        wd_h, wd_l = (sc.sb(n, [P, HT, DM], F32R) for n in ("wd_h", "wd_l"))
        da_h, da_l = (sc.sb(n, [P, HT, P], F32R) for n in ("da_h", "da_l"))
        au_h, au_l, ag_h, ag_l = (sc.sb(n, [P, KT, P], F32R) for n in ("au_h", "au_l", "ag_h", "ag_l"))
        db_h, db_l = (sc.sb(n, [P, DM], F32R) for n in ("db_h", "db_l"))
        al = slice(None)

        def by_tiles(src):
            full = HID // P
            return [((al, slice(0, full), al), src[0:full * P, :].rearrange("(t p) n -> p t n", p=P)),
                    ((slice(0, HID - full * P), full, al), src[full * P:HID, :])]

        split_on_chip(nc, "ffw1", [
            ("au", au_h, au_l, [((al, al, al), d["up_a"])]),
            ("ag", ag_h, ag_l, [((al, al, al), d["gate_a"])]),
            ("wu", wu_h, wu_l, [((al, al, slice(0, HID)), d["w_up"])]),
            ("wg", wg_h, wg_l, [((al, al, slice(0, HID)), d["w_gate2"])]),
            ("bu", bu_h, bu_l, [((al, slice(0, HID)), d["up_b"])]),
            ("bg", bg_h, bg_l, [((al, slice(0, HID)), d["gate_b"])]),
            ("da", da_h, da_l, by_tiles(d["down_a"])),
            ("wd", wd_h, wd_l, by_tiles(d["w_down"])),
            ("db", db_h, db_l, [((al, al), d["down_b"])]),
        ])
        x2h = [sc.sb(f"x2h{k}", [P, KT, BLK], F32R) for k in range(2)]
        x2l = [sc.sb(f"x2l{k}", [P, KT, BLK], F32R) for k in range(2)]
        msk = [sc.sb(f"msk{k}", [P, 2, BLK]) for k in range(2)]
        mdif = [sc.sb(f"mdif{k}", [P, BLK]) for k in range(2)]
        wbc = [sc.sb(f"wbc{k}", [P, 2, BLK]) for k in range(2)]
        xo = [sc.sb(f"xo{k}", [P, TPB, DM]) for k in range(2)]
        am_h = [sc.sb(f"am_h{k}", [P, 4, BLK], F32R) for k in range(2)]
        am_l = [sc.sb(f"am_l{k}", [P, 4, BLK], F32R) for k in range(2)]
        am_f = [sc.sb(f"am_f{k}", [P, BLK]) for k in range(2)]
        ch_f = [[sc.sb(f"ch_f{r}{j}", [P, BLK]) for j in range(2)] for r in range(2)]
        ch_h = [[sc.sb(f"ch_h{r}{j}", [P, BLK], F32R) for j in range(2)] for r in range(2)]
        ch_l = [[sc.sb(f"ch_l{r}{j}", [P, BLK], F32R) for j in range(2)] for r in range(2)]
        mix_f = [sc.sb(f"mix_f{j}", [P, BLK]) for j in range(4)]
        mix_h, mix_l = (sc.sb(n, [P, HT, BLK], F32R) for n in ("mix_h", "mix_l"))
        z_f = [sc.sb(f"z_f{r}", [P, BLK]) for r in range(2)]
        z_h, z_l = sc.sb("z_h", [P, BLK], F32R), sc.sb("z_l", [P, BLK], F32R)
        ps_u = [sc.bank(f"ps_u{j}") for j in range(2)]
        ps_g = [sc.bank(f"ps_g{j}") for j in range(2)]
        ps_d = [sc.bank(f"ps_d{r}") for r in range(2)]
        ps_a = [sc.bank(f"ps_a{b}") for b in range(2)]
        x2_in, msk_in, w_in, x1_in, out_done = (
            [sc.sem(f"{n}{k}") for k in range(2)] for n in ("x2_in", "msk_in", "w_in", "x1_in", "out_done"))
        ax_done, mdif_done, amf_done, amh_done, aml_done = (
            sc.sem(n) for n in ("ax_done", "mdif_done", "amf_done", "amh_done", "aml_done"))
        ug0_done, ug1_done, s0_done, s1_done, p0_done, p1_done = (
            sc.sem(n) for n in ("ug0_done", "ug1_done", "s0_done", "s1_done", "p0_done", "p1_done"))
        chf_done, chh_done, chl_done, mixf_done, mixh_done, mixl_done, da_done = (
            sc.sem(n) for n in ("chf_done", "chh_done", "chl_done", "mixf_done", "mixh_done", "mixl_done",
                                "da_done"))
        zp_done, zf_done, zh_done, zl_done, fin_done, fin_evac = (
            sc.sem(n) for n in ("zp_done", "zf_done", "zh_done", "zl_done", "fin_done", "fin_evac"))
        STEPS = NBLK * HT
        block = ctx.enter_context(nc.Block())

        def mix_slot(h, k):
            return (HT * k + h) % 4

        def walk(eng, step):
            def blocks(n, k):
                for h in range(HT):
                    step(n, h, k)
            for n in range(2):
                blocks(n, n % 2)
            with eng.Fori(1, NBLK // 2 - 1) as q:
                for k in range(2):
                    blocks(q * 2 + k, k)
            for n in range(NBLK - 2, NBLK + 1):
                blocks(n, n % 2)

        def live(n, end):
            return not isinstance(n, int) or 0 <= n < end

        @block.sync
        def _(sp):
            def load(n, k):
                cols = bass.ds(n * BLK, BLK)
                at_least(sp, ug0_done, HT * (n - 1))
                for dst, src in ((x2h, "x2h"), (x2l, "x2l")):
                    sp.dma_start(f32(dst[k][:]), d[src][bass.ds(n, 1)].rearrange("n p k l -> p (n k) l")
                                 ).then_inc(x2_in[k], 16)
                at_least(sp, zp_done, 2 * (n - 1))
                for r in range(2):
                    for e in range(E):
                        sp.dma_start(msk[k][e * R:(e + 1) * R, r, :],
                                     d["hot"][r * E + e, cols].partition_broadcast(R)).then_inc(msk_in[k], 16)
                at_least(sp, chf_done, 2 * HT * (n - 1))
                sp.dma_start(wbc[k][:], d["soft"][:, cols].partition_broadcast(P)).then_inc(w_in[k], 16)

            def store(n, k):
                for b in range(2):
                    sp.wait_ge(fin_evac, 2 * n + b + 1)
                    sp.dma_start(d["out"][bass.ds(n * 2 + b, 1)].rearrange("s (c p) d -> p (s c) d", p=P),
                                 xo[k][:, 2 * b:2 * b + 2, :]).then_inc(out_done[k], 16)

            def load_x1(n, k):
                at_least(sp, out_done[k], 16 * (n - k))
                sp.dma_start(xo[k][:], d["x1"][:, bass.ds(n * TPB, TPB), :]).then_inc(x1_in[k], 16)

            for n in range(2):
                load(n, n)
                load_x1(n, n)
            for n in range(2, 4):
                store(n - 2, n % 2)
                load(n, n % 2)
                load_x1(n, n % 2)
            with sp.Fori(2, NBLK // 2) as q:
                for k in range(2):
                    n = q * 2 + k
                    store(n - 2, k)
                    load(n, k)
                    load_x1(n, k)
            for n in range(NBLK - 2, NBLK):
                store(n, n % 2)
            for k in range(2):
                sp.wait_ge(out_done[k], 16 * NBLK)

        @block.tensor
        def _(pe):
            def a_x(n, k):
                pe.wait_ge(x2_in[k], 16 * (n - k) + 32)
                for b, (w_h, w_l) in enumerate(((au_h, au_l), (ag_h, ag_l))):
                    at_least(pe, fin_evac, 2 * (n - 2) + b + 1)
                    at_least(pe, amf_done, 4 * n)
                    for kt in range(KT):
                        last = three_passes(pe, ps_a[b][:], w_h[:, kt, :], w_l[:, kt, :],
                                            x2h[k][:, kt, :], x2l[k][:, kt, :], kt == 0, kt == KT - 1)
                    last.then_inc(ax_done, 1)

            def output(n, k):
                pe.wait_ge(mixl_done, HT * (n + 1))
                pe.wait_ge(zl_done, n + 1)
                for b in range(2):
                    for q in (2 * b, 2 * b + 1):
                        tok = slice(q * P, (q + 1) * P)
                        out = ps_a[b][:, (q % 2) * DM:(q % 2 + 1) * DM]
                        for h in range(HT):
                            three_passes(pe, out, mix_h[:, h, tok], mix_l[:, h, tok],
                                         wd_h[:, h, :], wd_l[:, h, :], h == 0, False)
                        last = three_passes(pe, out, z_h[:, tok], z_l[:, tok], db_h[:], db_l[:], False, True)
                    last.then_inc(fin_done, 1)

            def step(n, h, k):
                c = n * HT + h
                if h == 4 and live(n - 1, NBLK):
                    if live(n, NBLK):
                        pe.wait_ge(amf_done, 4 * (n + 1))
                    output(n - 1, 1 - k)
                if h == 5 and live(n + 1, NBLK):
                    a_x(n + 1, 1 - k)
                hid = slice(h * P, (h + 1) * P)
                if live(c, STEPS):
                    j = h % 2
                    for out, w_h, w_l, b_h, b_l, a, read in (
                            (ps_u[j], wu_h, wu_l, bu_h, bu_l, 0, s1_done),
                            (ps_g[j], wg_h, wg_l, bg_h, bg_l, 1, p1_done)):
                        at_least(pe, read, c - 1)
                        for kt in range(KT):
                            three_passes(pe, out[:], w_h[:, kt, hid], w_l[:, kt, hid],
                                         x2h[k][:, kt, :], x2l[k][:, kt, :], kt == 0, False)
                        pe.wait_ge(aml_done, 4 * n + a + 1)
                        last = three_passes(pe, out[:], b_h[:, hid], b_l[:, hid],
                                            am_h[k][:, a, :], am_l[k][:, a, :], False, True)
                    last.then_inc(ug0_done, 1)
                if live(c - 1, STEPS):
                    hh = (h - 1) % HT
                    nn, kk = (n, k) if h >= 1 else (n - 1, 1 - k)
                    prev = slice(hh * P, (hh + 1) * P)
                    pe.wait_ge(p0_done, c)
                    pe.wait_ge(aml_done, 4 * (nn + 1))
                    for out, b_h, b_l, a in ((ps_u[hh % 2], bu_h, bu_l, 2), (ps_g[hh % 2], bg_h, bg_l, 3)):
                        last = three_passes(pe, out[:], b_h[:, prev], b_l[:, prev],
                                            am_h[kk][:, a, :], am_l[kk][:, a, :], False, True, True)
                    last.then_inc(ug1_done, 1)
                if live(c - 2, STEPS):
                    hh = (h - 2) % HT
                    nn = n if h >= 2 else n - 1
                    if hh == 0:
                        at_least(pe, zp_done, 2 * nn)
                    for r in range(2):
                        pe.wait_ge(chl_done, 2 * (c - 2) + r + 1)
                        last = three_passes(pe, ps_d[r][:], da_h[:, hh, :], da_l[:, hh, :],
                                            ch_h[r][hh % 2][:], ch_l[r][hh % 2][:], hh == 0, hh == HT - 1)
                    last.then_inc(da_done, 1)

            a_x(0, 0)
            walk(pe, step)

        @block.scalar
        def _(act):
            def split_am(n, k, parts):
                for a in parts:
                    act.wait_ge(amf_done, 4 * n + a + 1)
                    at_least(act, ug1_done, HT * (n - 1))
                    act.activation(am_h[k][:, a, :], am_f[a % 2][:], ACT.Copy).then_inc(amh_done, 1)

            def step(n, h, k):
                c = n * HT + h
                j = h % 2
                if live(c - 2, STEPS):
                    for r in range(2):
                        act.wait_ge(chf_done, 2 * (c - 2) + r + 1)
                        at_least(act, da_done, c - 3)
                        act.activation(ch_h[r][j][:], ch_f[r][j][:], ACT.Copy).then_inc(chh_done, 1)
                if h == 3 and live(n - 1, NBLK):
                    act.wait_ge(zf_done, n)
                    at_least(act, fin_done, 2 * (n - 1))
                    act.activation(z_h[:], z_f[0][:], ACT.Copy).then_inc(zh_done, 1)
                if h == 5 and live(n + 1, NBLK):
                    split_am(n + 1, 1 - k, (0, 1))
                if h == 0 and live(n, NBLK):
                    split_am(n, k, (2, 3))
                if live(c - 4, STEPS):
                    hh = (h - 4) % HT
                    nn = n if h >= 4 else n - 1
                    act.wait_ge(mixf_done, c - 3)
                    at_least(act, fin_done, 2 * nn)
                    act.activation(mix_h[:, hh, :], mix_f[mix_slot(h, k)][:], ACT.Copy).then_inc(mixh_done, 1)
                if live(c, STEPS):
                    act.wait_ge(ug0_done, c + 1)
                    at_least(act, chl_done, 2 * (c - 1))
                    at_least(act, mixf_done, c - 1)
                    act.activation(ch_f[0][j][:], ps_u[j][:], ACT.Silu).then_inc(s0_done, 1)
                if live(c - 1, STEPS):
                    act.wait_ge(ug1_done, c)
                    act.activation(ch_f[1][1 - j][:], ps_u[1 - j][:], ACT.Silu).then_inc(s1_done, 1)

            split_am(0, 0, (0, 1))
            walk(act, step)

        @block.gpsimd
        def _(pool):
            def mask_difference(n, k):
                pool.wait_ge(msk_in[k], 128 * (n - k) + 256)
                at_least(pool, amf_done, 4 * (n - 1))
                pool.tensor_tensor(mdif[k][:], msk[k][:, 1, :], msk[k][:, 0, :], ALU.subtract
                                   ).then_inc(mdif_done, 1)

            def step(n, h, k):
                c = n * HT + h
                if h == 2 and live(n - 1, NBLK):
                    pool.wait_ge(zp_done, 2 * n)
                    pool.tensor_tensor(z_f[0][:], z_f[0][:], z_f[1][:], ALU.add).then_inc(zf_done, 1)
                if h == 4 and live(n + 1, NBLK):
                    mask_difference(n + 1, 1 - k)
                if live(c - 1, STEPS):
                    j = (h - 1) % 2
                    kk = k if h >= 1 else 1 - k
                    nn = n if h >= 1 else n - 1
                    if h == 1:
                        pool.wait_ge(w_in[kk], 8 * (nn - kk) + 16)
                    for r, done in ((0, p0_done), (1, p1_done)):
                        pool.wait_ge(done, c)
                        pool.tensor_tensor(ch_f[r][j][:], ch_f[r][j][:], wbc[kk][:, r, :], ALU.mult
                                           ).then_inc(chf_done, 1)
                    pool.wait_ge(chf_done, 2 * c)
                    at_least(pool, mixl_done, c - 4)
                    pool.tensor_tensor(mix_f[(mix_slot(h, k) - 1) % 4][:], ch_f[0][j][:], ch_f[1][j][:], ALU.add
                                       ).then_inc(mixf_done, 1)

            mask_difference(0, 0)
            walk(pool, step)

        @block.vector
        def _(v):
            def masked_ax(n, k, parts):
                for a in parts:
                    b = a % 2
                    mask = msk[k][:, 0, :] if a < 2 else mdif[k][:]
                    v.wait_ge(ax_done, 2 * n + b + 1)
                    at_least(v, aml_done, 4 * n + a - 1)
                    v.scalar_tensor_tensor(am_f[b][:], ps_a[b][:], LORA_ALPHA, mask, ALU.mult, ALU.mult
                                           ).then_inc(amf_done, 1)
                for a in parts:
                    v.wait_ge(amh_done, 4 * n + a + 1)
                    v.tensor_tensor(am_l[k][:, a, :], am_f[a % 2][:], f32(am_h[k][:, a, :]), ALU.subtract
                                    ).then_inc(aml_done, 1)

            def step(n, h, k):
                c = n * HT + h
                j = h % 2
                if live(c - 2, STEPS):
                    for r in range(2):
                        v.wait_ge(chh_done, 2 * (c - 2) + r + 1)
                        v.tensor_tensor(ch_l[r][j][:], ch_f[r][j][:], f32(ch_h[r][j][:]), ALU.subtract
                                        ).then_inc(chl_done, 1)
                if h == 2 and live(n - 1, NBLK):
                    m, kk = n - 1, 1 - k
                    v.wait_ge(da_done, HT * n)
                    at_least(v, zl_done, m)
                    for r in range(2):
                        v.scalar_tensor_tensor(z_f[r][:], ps_d[r][:], LORA_ALPHA, msk[kk][:, r, :], ALU.mult, ALU.mult
                                               ).then_inc(zp_done, 1)
                if h == 4 and live(n - 1, NBLK):
                    m, kk = n - 1, 1 - k
                    v.wait_ge(x1_in[kk], 8 * (m - kk) + 16)
                    for b in range(2):
                        v.wait_ge(fin_done, 2 * m + b + 1)
                        two = xo[kk][:, 2 * b:2 * b + 2, :]
                        v.tensor_tensor(two, ps_a[b][:].rearrange("p (q d) -> p q d", q=2), two, ALU.add
                                        ).then_inc(fin_evac, 1)
                if h == 5 and live(n + 1, NBLK):
                    v.wait_ge(msk_in[1 - k], 128 * (n + 1 - (1 - k)) + 256)
                    masked_ax(n + 1, 1 - k, (0, 1))
                if h == 0 and live(n, NBLK):
                    v.wait_ge(mdif_done, n + 1)
                    masked_ax(n, k, (2, 3))
                if h == 3 and live(n - 1, NBLK):
                    v.wait_ge(zh_done, n)
                    v.tensor_tensor(z_l[:], z_f[0][:], f32(z_h[:]), ALU.subtract).then_inc(zl_done, 1)
                if live(c - 4, STEPS):
                    hh = (h - 4) % HT
                    v.wait_ge(mixh_done, c - 3)
                    v.tensor_tensor(mix_l[:, hh, :], mix_f[mix_slot(h, k)][:], f32(mix_h[:, hh, :]), ALU.subtract
                                    ).then_inc(mixl_done, 1)
                if live(c, STEPS):
                    v.wait_ge(s0_done, c + 1)
                    v.tensor_tensor(ch_f[0][j][:], ps_g[j][:], ch_f[0][j][:], ALU.mult).then_inc(p0_done, 1)
                if live(c - 1, STEPS):
                    v.wait_ge(s1_done, c)
                    v.tensor_tensor(ch_f[1][1 - j][:], ps_g[1 - j][:], ch_f[1][1 - j][:], ALU.mult
                                    ).then_inc(p1_done, 1)

            v.wait_ge(msk_in[0], 256)
            masked_ax(0, 0, (0, 1))
            walk(v, step)


def program(nc, d):
    before = len(Scope.over)
    with ExitStack() as ctx:
        sc = Scope(nc, ctx, "k")
        keep = {"x": sc.sb("x", [P, TILES, DM]), "mean": sc.sb("mean", [P, TILES]),
                "rstd": sc.sb("rstd", [P, TILES])}
        stage_load_and_moments(nc, d, keep)
        with ExitStack() as mix:
            sm = Scope(nc, mix, "m")
            keep["xh"] = sm.sb("xh", [P, KT, TOK], F32R)
            keep["xl"] = sm.sb("xl", [P, KT, TOK], F32R)
            keep["cumT"] = sm.sb("cumT", [P, TILES, H])
            with ExitStack() as early:
                keep["dt"] = Scope(nc, early, "e").sb("dt", [H, TOK])
                stage_values(nc, d, keep)
                stage_decay(nc, d, keep)
            nc.clear_and_free_semaphores(Scope.over[before:])
            nc.all_engine_barrier()
            stage_mixer(nc, d, keep)
            stage_mixer_out(nc, d, keep)
        stage_route(nc, d, keep)
    stage_experts(nc, d)


def kernel(**inputs):
    import numpy as np
    import concourse.bacc as bacc
    from concourse.bass_utils import run_bass_kernel_spmd

    a = {n[3:]: np.asarray(v) for n, v in inputs.items()}
    w = a["attn_W_in"]
    bc = w[2 * DI:2 * DI + 2 * H * N].reshape(2, H, N, KT, P)

    def by_k(m):
        return np.ascontiguousarray(m.T.reshape(-1, P, m.shape[0]).transpose(1, 0, 2))

    arrays = {
        "x": a["attn_x"],
        "w_val": by_k(w[:DI]),
        "w_gate": by_k(w[DI:2 * DI]),
        "w_dt": by_k(w[2 * DI + 2 * H * N:]),
        "w_bc": np.ascontiguousarray(bc.transpose(1, 4, 3, 0, 2)).reshape(H, P, KT, 2 * N),
        "taps": np.ascontiguousarray(a["attn_conv_w"].reshape(CT, P, TAPS).transpose(1, 0, 2)),
        "conv_b": np.ascontiguousarray(a["attn_conv_b"].reshape(CT, P).T),
        "d_param": np.ascontiguousarray(a["attn_D_param"].reshape(GROUPS, GCH).T),
        "dt_bias": a["attn_dt_bias"].reshape(H, 1),
        "a_log": a["attn_A_log"].reshape(H, 1),
        "w_out": by_k(a["attn_W_out"]),
        "w_route": by_k(a["ffn_gate_w"]),
        "w_up": by_k(a["ffn_w_up"]),
        "w_gate2": by_k(a["ffn_w_gate"]),
        "w_down": np.ascontiguousarray(a["ffn_w_down"].T),
        "up_a": by_k(a["ffn_up_A"].reshape(E * R, DM)),
        "gate_a": by_k(a["ffn_gate_A"].reshape(E * R, DM)),
        "up_b": np.ascontiguousarray(a["ffn_up_B"].transpose(0, 2, 1).reshape(E * R, HID)),
        "gate_b": np.ascontiguousarray(a["ffn_gate_B"].transpose(0, 2, 1).reshape(E * R, HID)),
        "down_a": np.ascontiguousarray(a["ffn_down_A"].reshape(E * R, HID).T),
        "down_b": np.ascontiguousarray(a["ffn_down_B"].transpose(0, 2, 1).reshape(E * R, DM)),
        "ident": np.eye(P, dtype=np.float32),
        "rank": np.ascontiguousarray(np.broadcast_to(np.arange(E, 0, -1, dtype=np.float32), (P, E))),
        "mask": np.where(np.arange(P)[None, :] >= np.arange(P)[:, None], 0.0, NEG).astype(np.float32),
    }
    nc = bacc.Bacc("TRN2", target_bir_lowering=False, num_devices=1)
    d = {n: nc.dram_tensor(n, v.shape, mybir.dt.from_np(v.dtype), kind="ExternalInput").ap()
         for n, v in arrays.items()}
    for n, shape, dt in (("vT", [DI, TOK], F32), ("val", [SEQS, GROUPS, P, CPS, GCH], F32),
                         ("cum", [H, TOK], F32), ("y", [GROUPS * SEQS, GCH, SEQ], F32), ("x1", [P, TILES, DM], F32),
                         ("x2h", [NBLK, P, KT, BLK], F32), ("x2l", [NBLK, P, KT, BLK], F32),
                         ("hot", [2 * E, TOK], F32), ("soft", [2, TOK], F32)):
        d[n] = nc.dram_tensor(f"{n}_scratch", shape, dt, kind="Internal").ap()
    d["out"] = nc.dram_tensor("out", [SEQS, SEQ, DM], F32, kind="ExternalOutput").ap()
    program(nc, d)
    r = run_bass_kernel_spmd(nc, [arrays], core_ids=[0])
    return r.results[0]["out"]
```

```python
import math
from contextlib import ExitStack

import concourse.bass as bass
from concourse import mybir

F32 = mybir.dt.float32
F32R = mybir.dt.float32r
ACT = mybir.ActivationFunctionType
ALU = mybir.AluOpType
AX_X = mybir.AxisListType.X

P = 128
SEQS, SEQ, DM = 16, 256, 256
TOK = SEQS * SEQ
TILES = TOK // P
KT = DM // P
H, HD, N = 32, 16, 128
DI = H * HD
CT = DI // P
TAPS = 4
GH = 4
GROUPS = H // GH
GCH = GH * HD
CPS = SEQ // P
BLK = 512
NBLK = TOK // BLK
TPB = BLK // P
E, R = 8, 16
HID = 704
HT = (HID + P - 1) // P
HP = HT * P
EPS = 1e-5
LORA_ALPHA = 2.0
NEG = -1.0e30


def f32(ap):
    return ap.bitcast(F32)


class Scope:

    over = []

    def __init__(self, nc, ctx, stage):
        self.nc, self.ctx, self.stage = nc, ctx, stage

    def sb(self, name, shape, dt=F32):
        return self.ctx.enter_context(self.nc.sbuf_tensor(f"{self.stage}_{name}", shape, dt))

    def bank(self, name):
        return self.ctx.enter_context(self.nc.psum_tensor(f"{self.stage}_{name}", [P, 512], F32))

    def sem(self, name):
        made = self.nc.alloc_semaphore(f"{self.stage}_{name}")
        self.over.append(made)
        return made


def three_passes(pe, out, wh, wl, xh, xl, start, stop, skip=False):
    pe.matmul(out, wh, xh, start=start, stop=False, skip_group_check=skip)
    pe.matmul(out, wh, xl, start=False, stop=False, skip_group_check=skip)
    return pe.matmul(out, wl, xh, start=False, stop=stop, skip_group_check=skip)


def at_least(eng, sem, value):
    if not isinstance(value, int) or value > 0:
        eng.wait_ge(sem, value)


def finish_moments(v, st, mean, rstd, stats_done, step, var_ready, root_done, rstd_done):
    v.wait_ge(stats_done, TILES)
    v.tensor_tensor(mean[:], st[:, :, 1], st[:, :, 4], ALU.add).then_inc(step, 1)
    v.tensor_tensor(rstd[:], st[:, :, 1], st[:, :, 4], ALU.subtract).then_inc(step, 1)
    v.wait_ge(step, 2)
    v.tensor_scalar(mean[:], mean[:], 0.5, None, ALU.mult).then_inc(step, 1)
    v.scalar_tensor_tensor(rstd[:], rstd[:], 0.25, rstd[:], ALU.mult, ALU.mult).then_inc(step, 1)
    v.tensor_tensor(st[:, :, 0], st[:, :, 2], st[:, :, 5], ALU.add).then_inc(step, 1)
    v.wait_ge(step, 5)
    v.scalar_tensor_tensor(rstd[:], st[:, :, 0], 1.0 / DM, rstd[:], ALU.mult, ALU.add).then_inc(step, 1)
    v.wait_ge(step, 6)
    v.tensor_scalar(rstd[:], rstd[:], EPS, None, ALU.add).then_inc(var_ready, 1)
    v.wait_ge(root_done, 1)
    v.reciprocal(rstd[:], rstd[:]).then_inc(rstd_done, 1)
    v.wait_ge(rstd_done, 1)


def stage_load_and_moments(nc, d, keep):
    with ExitStack() as ctx:
        sc = Scope(nc, ctx, "ln1")
        x_sb, mean, rstd = keep["x"], keep["mean"], keep["rstd"]
        st = sc.sb("st", [P, TILES, 6])
        al = slice(None)
        weights = Weights(sc, "w", [("val", keep["wv_h"], keep["wv_l"],
                                     [((al, al, slice(0, DI)), d["w_val"]),
                                      ((al, al, slice(DI, DI + 2 * H)), d["w_dt"])])])
        x_in = [sc.sem(f"x_in{c}") for c in range(8)]
        stats_done, step, var_ready, root_done, rstd_done = (
            sc.sem(n) for n in ("stats_done", "step", "var_ready", "root_done", "rstd_done"))
        block = ctx.enter_context(nc.Block())

        @block.sync
        def _(sp):
            xv = d["x"].rearrange("s (c p) d -> p (s c) d", p=P)
            for c in range(8):
                if c == 4:
                    weights.load(sp)
                sp.dma_start(x_sb[:, 4 * c:4 * c + 4, :], xv[:, 4 * c:4 * c + 4, :]).then_inc(x_in[c], 16)

        @block.gpsimd
        def _(pool):
            weights.zero(pool)
            weights.split_lo(pool)

        @block.vector
        def _(v):
            for c in range(8):
                v.wait_ge(x_in[c], 16)
                for t in range(4 * c, 4 * c + 4):
                    v.bn_stats(st[:, t, :], x_sb[:, t, :]).then_inc(stats_done, 1)
            finish_moments(v, st, mean, rstd, stats_done, step, var_ready, root_done, rstd_done)

        @block.scalar
        def _(act):
            weights.split_hi(act)
            act.wait_ge(var_ready, 1)
            act.activation(rstd[:], rstd[:], ACT.Sqrt).then_inc(root_done, 1)


def stage_values(nc, d, keep):
    with ExitStack() as ctx:
        sc = Scope(nc, ctx, "val")
        x_sb, mean, rstd, xh, xl, dt_raw = (keep[n] for n in ("x", "mean", "rstd", "xh", "xl", "dt"))
        w_h, w_l = keep["wv_h"], keep["wv_l"]
        taps = sc.sb("taps", [P, CT, TAPS])
        conv_b = sc.sb("conv_b", [P, CT])
        dt_bias = sc.sb("dt_bias", [2 * H, 1])
        ident = sc.sb("ident", [P, P])
        xn = [sc.sb(f"xn{k}", [P, CPS, DM]) for k in range(2)]
        vbuf = [sc.sb(f"vbuf{k}", [P, CT, TAPS - 1 + SEQ]) for k in range(2)]
        acc = [sc.sb(f"acc{k}", [P, CT, SEQ]) for k in range(2)]
        vs, vtok = keep["vs"], keep["vtok"]
        ps_t = [sc.bank(f"ps_t{k}") for k in range(2)]
        ps_v = [sc.bank(f"ps_v{k}") for k in range(2)]
        ps_dt = sc.bank("ps_dt")
        ps_o = [sc.bank(f"ps_o{k}") for k in range(2)]
        small_in, pad_ready = sc.sem("small_in"), sc.sem("pad_ready")
        xn_ready, tr_done, xhi_done, xlo_done = (
            sc.sem(n) for n in ("xn_ready", "tr_done", "xhi_done", "xlo_done"))
        v_done, v_evac, dt_done, dt_evac, conv_step, silu_done = (
            sc.sem(n) for n in ("v_done", "v_evac", "dt_done", "dt_evac", "conv_step", "silu_done"))
        vt_done, vtok_c0, vtok_c1 = (sc.sem(n) for n in ("vt_done", "vtok_c0", "vtok_c1"))
        vT_out = [sc.sem(f"vT_out{k}") for k in range(2)]
        vtok_out = [sc.sem(f"vtok_out{k}") for k in range(2)]
        PC = CT - 1
        STEPS = PC * (TAPS - 1)
        PSTEPS = 2 * (TAPS - 1)
        tapped = sc.sb("tapped", [P, SEQ])
        pconv_step = sc.sem("pconv_step")
        block = ctx.enter_context(nc.Block())

        def slots(eng, slot):
            for s in range(4):
                slot(s, s % 2)
            with eng.Fori(2, SEQS // 2 - 1) as q:
                for k in range(2):
                    slot(q * 2 + k, k)
            for s in range(SEQS - 2, SEQS + 3):
                slot(s, s % 2)

        def live(n):
            return not isinstance(n, int) or 0 <= n < SEQS

        def starts(s):
            return not isinstance(s, int) or s < SEQS

        @block.sync
        def _(sp):
            for dst, src in ((ident, "ident"), (taps, "taps"), (conv_b, "conv_b"), (dt_bias, "dt_bias")):
                sp.dma_start(dst[:], d[src]).then_inc(small_in, 16)

            vT_view = d["vT"].rearrange("(c p) l -> p c l", p=P)

            def slot(s, k):
                m = s - 2
                if live(m):
                    sp.wait_ge(silu_done, m + 1)
                    sp.dma_start(vT_view[:, :, bass.ds(m * SEQ, SEQ)], vs[k][:]).then_inc(vT_out[k], 16)
                if live(m - 1):
                    sp.wait_ge(vtok_c0, m)
                    sp.wait_ge(vtok_c1, m)
                    sp.dma_start(d["val"][bass.ds(m - 1, 1)].rearrange("s p c q -> p (s c) q"), vtok[1 - k][:]
                                 ).then_inc(vtok_out[1 - k], 16)
            slots(sp, slot)
            keep["stores"] = [(vT_out[k], 16 * (SEQS // 2)) for k in range(2)] + [
                (vtok_out[k], 16 * (SEQS // 2)) for k in range(2)]

        @block.gpsimd
        def _(pool):
            for k in range(2):
                pool.memset(vbuf[k][:, :, 0:TAPS - 1], 0.0).then_inc(pad_ready, 1)
            pool.wait_ge(small_in, 64)

            def slot(s, k):
                n, j = s - 1, 1 - k
                if live(n):
                    for tap in range(TAPS - 1):
                        if tap == 0:
                            pool.wait_ge(v_evac, 2 * n + 2)
                        at_least(pool, pconv_step, PSTEPS * n + 2 * tap)
                        pool.tensor_tensor(tapped[:], vbuf[j][:, PC, tap:tap + SEQ],
                                           taps[:, PC, tap:tap + 1].broadcast_to([P, SEQ]), ALU.mult
                                           ).then_inc(pconv_step, 1)
                        pool.wait_ge(pconv_step, PSTEPS * n + 2 * tap + 1)
                        pool.tensor_tensor(acc[j][:, PC, :], acc[j][:, PC, :], tapped[:], ALU.add
                                           ).then_inc(pconv_step, 1)
            slots(pool, slot)

        @block.tensor
        def _(pe):
            pe.wait_ge(small_in, 64)

            def slot(s, k):
                n, o = s - 1, s - 3
                if starts(s):
                    at_least(pe, xlo_done, s - 1)
                    pe.wait_ge(xn_ready, s + 1)
                    for kt in range(KT):
                        for c in range(CPS):
                            last = pe.transpose(ps_t[k][:, kt * SEQ + c * P:kt * SEQ + (c + 1) * P],
                                                xn[k][:, c, kt * P:(kt + 1) * P], ident[:])
                    last.then_inc(tr_done, 1)
                if live(n):
                    pe.wait_ge(xlo_done, n + 1)
                    cols = bass.ds(n * SEQ, SEQ)
                    for b in range(2):
                        at_least(pe, v_evac, 2 * n + b - 1)
                        for ct in (2 * b, 2 * b + 1):
                            out = ps_v[b][:, (ct % 2) * SEQ:(ct % 2 + 1) * SEQ]
                            ch = slice(ct * P, (ct + 1) * P)
                            for kt in range(KT):
                                last = three_passes(pe, out, w_h[:, kt, ch], w_l[:, kt, ch],
                                                    xh[:, kt, cols], xl[:, kt, cols],
                                                    kt == 0, kt == KT - 1)
                        last.then_inc(v_done, 1)
                    at_least(pe, dt_evac, n)
                    for kt in range(KT):
                        last = three_passes(pe, ps_dt[:, 0:SEQ], w_h[:, kt, DI:], w_l[:, kt, DI:],
                                            xh[:, kt, cols], xl[:, kt, cols], kt == 0, kt == KT - 1)
                    last.then_inc(dt_done, 1)
                if live(o):
                    pe.wait_ge(silu_done, o + 1)
                    for c, evac in ((0, vtok_c0), (1, vtok_c1)):
                        at_least(pe, evac, o)
                        for ct in range(CT):
                            last = pe.transpose(ps_o[c][:, ct * P:(ct + 1) * P],
                                                vs[1 - k][:, ct, c * P:(c + 1) * P], ident[:])
                        last.then_inc(vt_done, 1)
            slots(pe, slot)

        @block.scalar
        def _(act):
            act.wait_ge(pad_ready, 2)
            act.wait_ge(small_in, 64)

            def slot(s, k):
                n, m = s - 1, s - 2
                if starts(s):
                    act.wait_ge(tr_done, s + 1)
                    act.activation(xh[:, :, bass.ds(s * SEQ, SEQ)],
                                   ps_t[k][:].rearrange("p (a b) -> p a b", a=KT), ACT.Copy
                                   ).then_inc(xhi_done, 1)
                if live(n):
                    j = 1 - k
                    at_least(act, conv_step, STEPS * (n - 1))
                    at_least(act, pconv_step, PSTEPS * (n - 1))
                    at_least(act, silu_done, n - 1)
                    for b in range(2):
                        act.wait_ge(v_done, 2 * n + b + 1)
                        act.activation(vbuf[j][:, 2 * b:2 * b + 2, TAPS - 1:],
                                       ps_v[b][:].rearrange("p (a b) -> p a b", a=2), ACT.Copy)
                        for ct in (2 * b, 2 * b + 1):
                            last = act.activation(acc[j][:, ct, :], ps_v[b][:, (ct % 2) * SEQ:(ct % 2 + 1) * SEQ],
                                                  ACT.Identity, bias=conv_b[:, ct:ct + 1],
                                                  scale=taps[:, ct, TAPS - 1:TAPS])
                        last.then_inc(v_evac, 1)
                    act.wait_ge(dt_done, n + 1)
                    rows = slice(H * j, H * (j + 1))
                    act.activation(dt_raw[rows, bass.ds((n - j) * (SEQ // 2), SEQ)], ps_dt[rows, 0:SEQ],
                                   ACT.Identity, bias=dt_bias[rows, 0:1]).then_inc(dt_evac, 1)
                if live(m):
                    act.wait_ge(conv_step, STEPS * (m + 1))
                    act.wait_ge(pconv_step, PSTEPS * (m + 1))
                    at_least(act, vT_out[k], 8 * (m - k))
                    at_least(act, vt_done, 2 * (m - 1))
                    act.activation(vs[k][:], acc[k][:], ACT.Silu).then_inc(silu_done, 1)
                if live(m - 1):
                    o, kk = m - 1, 1 - k
                    act.wait_ge(vt_done, 2 * o + 1)
                    at_least(act, vtok_out[kk], 8 * (o - kk))
                    act.activation(vtok[kk][:, 0, :], ps_o[0][:], ACT.Copy).then_inc(vtok_c0, 1)
            slots(act, slot)

        @block.vector
        def _(v):

            def normalise(s, k):
                at_least(v, tr_done, s - 1)
                for c in range(CPS):
                    t = s * CPS + c
                    last = v.tensor_scalar(xn[k][:, c, :], x_sb[:, bass.ds(t, 1), :], mean[:, bass.ds(t, 1)],
                                           rstd[:, bass.ds(t, 1)], ALU.subtract, ALU.mult)
                last.then_inc(xn_ready, 1)

            def slot(s, k):
                n = s - 1
                if starts(s):
                    v.wait_ge(xhi_done, s + 1)
                    cols = bass.ds(s * SEQ, SEQ)
                    v.tensor_tensor(xl[:, :, cols], ps_t[k][:].rearrange("p (a b) -> p a b", a=KT),
                                    f32(xh[:, :, cols]), ALU.subtract).then_inc(xlo_done, 1)
                if starts(s + 1):
                    normalise(s + 1, 1 - k)
                if live(n):
                    j = 1 - k
                    v.wait_ge(v_evac, 2 * n + 2)
                    for tap in range(TAPS - 1):
                        for ct in range(PC):
                            if tap:
                                v.wait_ge(conv_step, STEPS * n + PC * (tap - 1) + ct + 1)
                            v.scalar_tensor_tensor(acc[j][:, ct, :], vbuf[j][:, ct, tap:tap + SEQ],
                                                   taps[:, ct, tap:tap + 1], acc[j][:, ct, :],
                                                   ALU.mult, ALU.add).then_inc(conv_step, 1)
                if live(s - 3):
                    o, kk = s - 3, 1 - k
                    v.wait_ge(vt_done, 2 * o + 2)
                    at_least(v, vtok_out[kk], 8 * (o - kk))
                    v.tensor_copy(vtok[kk][:, 1, :], ps_o[1][:]).then_inc(vtok_c1, 1)
            normalise(0, 0)
            v.wait_ge(small_in, 64)
            slots(v, slot)


def stage_decay(nc, d, keep):
    with ExitStack() as ctx:
        sc = Scope(nc, ctx, "dec")
        dt, cumT = keep["dt"], keep["cumT"]
        az, ex, cum, carry = (sc.sb(n, [2 * H, TOK // 2]) for n in ("az", "ex", "cum", "carry"))
        a_log, na, ident = sc.sb("a_log", [2 * H, 1]), sc.sb("na", [2 * H, 1]), sc.sb("ident", [2 * H, 2 * H])
        ps = [sc.bank(f"ps{b}") for b in range(2)]
        small_in, ones, carry_ready, a_exp, na_done = (
            sc.sem(n) for n in ("small_in", "ones", "carry_ready", "a_exp", "na_done"))
        az_done, ex_done, ln_done, sp_done, ld_done, cum_done, tr_done, cumT_done, cum_out = (
            sc.sem(n) for n in ("az_done", "ex_done", "ln_done", "sp_done", "ld_done", "cum_done",
                                "tr_done", "cumT_done", "cum_out"))
        CH = 4
        W = TOK // 2 // CH
        HALF = TOK // 4 // P
        part = [slice(c * W, (c + 1) * W) for c in range(CH)]
        block = ctx.enter_context(nc.Block())

        @block.sync
        def _(sp):
            sp.dma_start(a_log[:], d["a_log"]).then_inc(small_in, 16)
            sp.dma_start(ident[:], d["ident"][0:2 * H, 0:2 * H]).then_inc(small_in, 16)
            by_parity = d["cum"].rearrange("h (s two l) -> two h s l", two=2, l=SEQ)
            pairs = W // SEQ
            for c in range(CH):
                sp.wait_ge(cum_done, c + 1)
                for odd in range(2):
                    sp.dma_start(by_parity[odd][:, c * pairs:(c + 1) * pairs, :],
                                 cum[odd * H:(odd + 1) * H, part[c]].rearrange("h (s l) -> h s l", l=SEQ)
                                 ).then_inc(cum_out, 16)
            for stored, value in keep["stores"]:
                sp.wait_ge(stored, value)
            sp.wait_ge(cum_out, 32 * CH)

        @block.gpsimd
        def _(pool):
            pool.memset(carry[:], 1.0).then_inc(ones, 1)
            pool.wait_ge(ones, 1)
            pool.memset(carry[:].rearrange("h (s l) -> h s l", l=SEQ)[:, :, 0:1], 0.0).then_inc(carry_ready, 1)

        @block.scalar
        def _(act):
            for c in range(CH):
                act.wait_ge(az_done, c + 1)
                act.activation(ex[:, part[c]], az[:, part[c]], ACT.Exp).then_inc(ex_done, 1)
            act.wait_ge(small_in, 32)
            act.activation(na[:], a_log[:], ACT.Exp).then_inc(a_exp, 1)
            for c in range(CH):
                act.wait_ge(ex_done, c + 1)
                act.activation(ex[:, part[c]], ex[:, part[c]], ACT.Ln, bias=1.0).then_inc(ln_done, 1)
            act.wait_ge(na_done, 1)
            for c in range(CH):
                act.wait_ge(sp_done, c + 1)
                act.activation(dt[:, part[c]], dt[:, part[c]], ACT.Copy, scale=na[:, 0:1]).then_inc(ld_done, 1)

        @block.vector
        def _(v):
            for c in range(CH):
                v.scalar_tensor_tensor(az[:, part[c]], dt[:, part[c]], -1.0, dt[:, part[c]],
                                       ALU.mult, ALU.min).then_inc(az_done, 1)
            v.wait_ge(a_exp, 1)
            v.tensor_scalar(na[:], na[:], -1.0, None, ALU.mult).then_inc(na_done, 1)
            v.wait_ge(carry_ready, 1)
            for c in range(CH + 1):
                if c < CH:
                    v.wait_ge(ln_done, c + 1)
                    v.scalar_tensor_tensor(dt[:, part[c]], dt[:, part[c]], 0.0, ex[:, part[c]],
                                           ALU.max, ALU.add).then_inc(sp_done, 1)
                if c >= 1:
                    v.wait_ge(ld_done, c)
                    v.tensor_tensor_scan(cum[:, part[c - 1]], carry[:, part[c - 1]], dt[:, part[c - 1]], 0.0,
                                         ALU.mult, ALU.add).then_inc(cum_done, 1)
            for b in range(2):
                v.wait_ge(tr_done, b + 1)
                for c in range(CPS):
                    v.tensor_copy(cumT[:, b * 16:(b + 1) * 16, :].rearrange(
                                      "p (s two c) h -> p s two c h", two=2, c=CPS)[:, :, :, c, :],
                                  ps[b][:].rearrange("p (s c two h) -> p s c two h", c=CPS, two=2, h=H)[:, :, c, :, :]
                                  ).then_inc(cumT_done, 1)

        @block.tensor
        def _(pe):
            pe.wait_ge(small_in, 32)
            for b in range(2):
                for t in range(HALF):
                    col = (b * HALF + t) * P
                    if col % W == 0:
                        pe.wait_ge(cum_done, col // W + 1)
                    last = pe.transpose(ps[b][:, t * 2 * H:(t + 1) * 2 * H], cum[:, col:col + P], ident[:])
                last.then_inc(tr_done, 1)


def stage_mixer(nc, d, keep):
    with ExitStack() as ctx:
        sc = Scope(nc, ctx, "mix")
        xh, xl, cumT = (keep[n] for n in ("xh", "xl", "cumT"))
        mask = sc.sb("mask", [P, P])
        weights = Weights(sc, "gate", [("w", keep["wg_h"], keep["wg_l"],
                                        [((slice(None), slice(None), slice(None)), d["w_gate"])])])
        w_raw = [sc.sb(f"w_raw{j}", [P, KT, 2 * N]) for j in range(GH)]
        w_h = [sc.sb(f"w_h{j}", [P, KT, 2 * N], F32R) for j in range(GH)]
        w_l = [sc.sb(f"w_l{j}", [P, KT, 2 * N], F32R) for j in range(GH)]
        cum = [sc.sb(f"cum{k}", [P, GH, SEQ]) for k in range(2)]
        vst = [sc.sb(f"vst{k}", [P, CPS, GCH]) for k in range(2)]
        vp = [sc.sb(f"vp{k}", [P, CPS, GH, 2, GCH], F32R) for k in range(2)]
        d_param = sc.sb("d_param", [GCH, GROUPS])
        vT = [sc.sb(f"vT{k}", [GCH, SEQ]) for k in range(2)]
        dv = [sc.sb(f"dv{k}", [GCH, SEQ]) for k in range(2)]
        y_lo = sc.sb("y_lo", [GCH, SEQ])
        LW = SEQ + P
        dec = [sc.sb(f"dec{k}", [P, GH, LW]) for k in range(2)]
        hl = [sc.sb(f"hl{k}", [P, P]) for k in range(2)]
        bc = [sc.sb(f"bc{k}", [P, 2, 2 * SEQ], F32R) for k in range(2)]
        m_f = [sc.sb(f"m_f{k}", [P, LW]) for k in range(2)]
        m_h = [sc.sb(f"m_h{k}", [P, LW], F32R) for k in range(4)]
        m_l = [sc.sb(f"m_l{k}", [P, LW], F32R) for k in range(4)]
        yst = [sc.sb(f"yst{k}", [GCH, SEQ]) for k in range(2)]
        ps_p = [sc.bank(f"ps_p{k}") for k in range(4)]
        ps_c = [sc.bank(f"ps_c{k}") for k in range(2)]
        ps_y = [sc.bank(f"ps_y{k}") for k in range(2)]
        small_in, zeroed = sc.sem("small_in"), sc.sem("zeroed")
        vT_in = [sc.sem(f"vT_in{k}") for k in range(2)]
        dv_done, ylo_done, yhi_done = sc.sem("dv_done"), sc.sem("ylo_done"), sc.sem("yhi_done")
        w_in = [sc.sem(f"w_in{j}") for j in range(GH)]
        cum_in = [sc.sem(f"cum_in{k}") for k in range(2)]
        v_in = [sc.sem(f"v_in{k}") for k in range(2)]
        y_out = [sc.sem(f"y_out{k}") for k in range(2)]
        w_hi, w_lo, hl_done, own_done = (sc.sem(n) for n in ("w_hi", "w_lo", "hl_done", "own_done"))
        dif_done, msk_done, vh_done, vp_done = (
            sc.sem(n) for n in ("dif_done", "msk_done", "vh_done", "vp_done"))
        p_done, bh_done, bl_done, c_done, exp_done = (
            sc.sem(n) for n in ("p_done", "bh_done", "bl_done", "c_done", "exp_done"))
        mt_done, mh_done, ml_done, pv_done, y_evac = (
            sc.sem(n) for n in ("mt_done", "mh_done", "ml_done", "pv_done", "y_evac"))
        ITERS = GROUPS * SEQS
        UNITS = GH * ITERS
        block = ctx.enter_context(nc.Block())

        def walk(eng, iteration, after_first=None, last=None):
            pairs = SEQS // 2 - (1 if last else 0)

            def end_of_group(g):
                if last:
                    s = SEQS - 2
                    iteration(g * SEQS + s, g, s, 0)
                    last(g * SEQS + s + 1, g, s + 1, 1)

            for i in range(4):
                if after_first and i == 2:
                    after_first(0)
                iteration(i, 0, i, i % 2)
            with eng.Fori(2, pairs) as q:
                for k in range(2):
                    iteration(q * 2 + k, 0, q * 2 + k, k)
            end_of_group(0)
            with eng.Fori(1, GROUPS) as g:
                if after_first:
                    for k in range(2):
                        iteration(g * SEQS + k, g, k, k)
                    after_first(g)
                with eng.Fori(1 if after_first else 0, pairs) as q:
                    for k in range(2):
                        s = q * 2 + k
                        iteration(g * SEQS + s, g, s, k)
                end_of_group(g)
            for i in range(ITERS, ITERS + 4):
                iteration(i, GROUPS - 1, i, i % 2)

        def live(n, end):
            return not isinstance(n, int) or 0 <= n < end

        @block.sync
        def _(sp):

            def load_weights(g):
                for j in range(GH):
                    at_least(sp, w_lo, g * GH + j - GH + 1)
                    sp.dma_start(w_raw[j][:], d["w_bc"][bass.ds((g % GROUPS) * GH + j, 1)].rearrange("h p k n -> p (h k) n")
                                 ).then_inc(w_in[j], 16)

            def iteration(i, g, s, k):
                if live(i, ITERS):
                    at_least(sp, msk_done, i - 1)
                    sp.dma_start(cum[k][:], d["cum"][bass.ds(g * GH, GH), bass.ds(s * SEQ, SEQ)]
                                 .partition_broadcast(P)).then_inc(cum_in[k], 16)
                    at_least(sp, vp_done, i - 1)
                    sp.dma_start(vst[k][:], d["val"][bass.ds(s, 1), :, :, bass.ds(g * GCH, GCH)]
                                 .rearrange("s p c q -> p (s c) q")).then_inc(v_in[k], 16)
                    at_least(sp, dv_done, i - 1)
                    sp.dma_start(vT[k][:], d["vT"][bass.ds(g * GCH, GCH), bass.ds(s * SEQ, SEQ)]
                                 ).then_inc(vT_in[k], 16)
                if live(i - 3, ITERS):
                    sp.wait_ge(y_evac, i - 2)
                    sp.dma_start(d["y"][bass.ds(i - 3, 1)].rearrange("i c l -> (i c) l"), yst[1 - k][:]
                                 ).then_inc(y_out[1 - k], 16)

            def next_weights(g):
                load_weights(g + 1)
                if isinstance(g, int):
                    weights.load(sp)

            load_weights(0)
            sp.dma_start(mask[:], d["mask"]).then_inc(small_in, 16)
            sp.dma_start(d_param[:], d["d_param"]).then_inc(small_in, 16)
            walk(sp, iteration, next_weights)
            for k in range(2):
                sp.wait_ge(y_out[k], 16 * (ITERS // 2))
            for j in range(GH):
                sp.wait_ge(w_in[j], 16 * (GROUPS + 1))

        @block.gpsimd
        def _(pool):
            for k in range(2):
                pool.memset(f32(vp[k][:]), 0.0).then_inc(zeroed, 1)
            weights.zero(pool)
            pool.wait_ge(zeroed, 2)
            pool.wait_ge(small_in, 32)

            def diag(k, part):
                return bass.AP(vp[k], part * GCH, [[CPS * GH * P, P], [GH * P, CPS], [P + HD, GH], [1, HD]])

            def iteration(i, g, s, k):
                if live(i, ITERS):
                    pool.wait_ge(cum_in[k], 8 * (i - k) + 16)
                    at_least(pool, mt_done, GH * (i - 1))
                    for c in range(CPS):
                        row = cumT[:, bass.ds(s * CPS + c, 1), bass.ds(g * GH, GH)].rearrange("p o h -> p (o h)")
                        w = SEQ if c == 0 else P
                        pool.tensor_tensor(dec[k][:, :, c * SEQ:c * SEQ + w], cum[k][:, :, c * P:c * P + w],
                                           row.unsqueeze(2).broadcast_to([P, GH, w]), ALU.subtract
                                           ).then_inc(dif_done, 1)
                    pool.wait_ge(dif_done, 2 * i + 2)
                    pool.wait_ge(v_in[k], 8 * (i - k) + 16)
                    at_least(pool, pv_done, GH * (i - 1))
                    tri = dec[k][:].rearrange("p h (b l) -> p h b l", l=P)[:, :, 0:3:2, :]
                    pool.tensor_tensor(tri, tri, mask[:].unsqueeze(1).unsqueeze(1).broadcast_to([P, GH, 2, P]),
                                       ALU.add).then_inc(msk_done, 1)
                    v4 = vst[k][:].rearrange("p c (h q) -> p c h q", q=HD)
                    pool.tensor_copy(diag(k, 0), v4).then_inc(vh_done, 1)
                    pool.wait_ge(vh_done, i + 1)
                    pool.tensor_tensor(diag(k, 1), v4, diag(k, 0).bitcast(F32), ALU.subtract
                                       ).then_inc(vp_done, 1)
            walk(pool, iteration)

        @block.tensor
        def _(pe):
            pe.wait_ge(zeroed, 2)

            def iteration(i, g, s, k):
                cols = None
                for j in range(GH):
                    t = i * GH + j
                    if live(i, ITERS):
                        pe.wait_ge(w_lo, g * GH + j + 1)
                        at_least(pe, bl_done, t - 3)
                        cols = bass.ds(s * SEQ, SEQ)
                        for b in range(2):
                            for kt in range(KT):
                                last = three_passes(
                                    pe, ps_p[j][:, b * SEQ:(b + 1) * SEQ],
                                    w_h[j][:, kt, b * N:(b + 1) * N], w_l[j][:, kt, b * N:(b + 1) * N],
                                    xh[:, kt, cols], xl[:, kt, cols], kt == 0, kt == KT - 1)
                        last.then_inc(p_done, 1)
                    if live(t - 2, UNITS):
                        pe.wait_ge(bl_done, t - 1)
                        at_least(pe, mt_done, t - 3)
                        hi, lo = bc[j % 2][:, 0, :], bc[j % 2][:, 1, :]
                        three_passes(pe, ps_c[j % 2][:, 0:SEQ], hi[:, 0:P], lo[:, 0:P],
                                     hi[:, SEQ:], lo[:, SEQ:], True, True)
                        pe.matmul(ps_c[j % 2][:, SEQ:], hi[:, P:SEQ], bc[j % 2][:, :, SEQ + P:],
                                  start=True, stop=False, skip_group_check=True)
                        pe.matmul(ps_c[j % 2][:, SEQ:LW], lo[:, P:SEQ], hi[:, SEQ + P:],
                                  start=False, stop=True, skip_group_check=True).then_inc(c_done, 1)
                    if live(t - 4, UNITS):
                        n, o = i - 1, 1 - k
                        if j == 0:
                            pe.wait_ge(vp_done, n + 1)
                            at_least(pe, y_evac, n - 1)
                        pe.wait_ge(ml_done, t - 3)
                        for c in range(CPS):
                            seen = slice(c * P, SEQ)
                            mine = slice(c * SEQ, c * SEQ + SEQ - c * P)
                            pe.matmul(ps_y[o][:, seen], vp[o][:, c, j, :, :].rearrange("p h q -> p (h q)"),
                                      m_h[j][:, mine], start=(j == 0 and c == 0), stop=False,
                                      skip_group_check=True)
                            last = pe.matmul(ps_y[o][0:GCH, seen], vp[o][:, c, j, 0, :], m_l[j][:, mine],
                                             start=False, stop=(j == GH - 1 and c == CPS - 1),
                                             skip_group_check=True)
                        last.then_inc(pv_done, 1)
            walk(pe, iteration)

        @block.scalar
        def _(act):
            act.wait_ge(small_in, 32)

            def split_weights(g, j):
                act.wait_ge(w_in[j], g * 16 + 16)
                act.activation(w_h[j][:], w_raw[j][:], ACT.Copy).then_inc(w_hi, 1)

            def last(i, g, s, k):
                iteration(i, g, s, k, True)

            def iteration(i, g, s, k, last=False):
                if live(i - 2, ITERS):
                    act.wait_ge(pv_done, GH * (i - 1))
                    at_least(act, y_evac, i - 2)
                    act.activation(y_lo[:], ps_y[k][GCH:, 0:SEQ], ACT.Copy).then_inc(ylo_done, 1)
                for j in range(GH):
                    t = i * GH + j
                    if live(t - 3, UNITS):
                        r = (j + 1) % 4
                        act.wait_ge(mt_done, t - 2)
                        at_least(act, pv_done, t - 6)
                        act.activation(m_h[r][:], m_f[(j + 1) % 2][:], ACT.Copy).then_inc(mh_done, 1)
                    if live(t - 2, UNITS):
                        act.wait_ge(c_done, t - 1)
                        at_least(act, own_done, t - 3)
                        act.activation(hl[j % 2][:], ps_c[j % 2][:, LW:], ACT.Copy).then_inc(hl_done, 1)
                    if live(i, ITERS):
                        act.wait_ge(p_done, t + 1)
                        at_least(act, c_done, t - 1)
                        if j == 3:
                            act.wait_ge(vT_in[k], 8 * (i - k) + 16)
                            at_least(act, yhi_done, i - 1)
                        act.activation(bc[j % 2][:, 0, :], ps_p[j][:], ACT.Copy).then_inc(bh_done, 1)
                        if j < 2:
                            act.wait_ge(msk_done, i + 1)
                            half = dec[k][:, 2 * j:2 * j + 2, :]
                            act.activation(half, half, ACT.Exp).then_inc(exp_done, 1)
                        if last:
                            split_weights(g + 1, j)
                        if j == 3:
                            act.activation(dv[k][:], vT[k][:], ACT.Copy, scale=d_param[:, bass.ds(g, 1)]
                                           ).then_inc(dv_done, 1)
            for j in range(GH):
                split_weights(0, j)
            walk(act, iteration, last=last)
            weights.split_hi(act)

        @block.vector
        def _(v):
            def split_weights(g, j):
                v.wait_ge(w_hi, g * GH + j + 1)
                v.tensor_tensor(w_l[j][:], w_raw[j][:], f32(w_h[j][:]), ALU.subtract).then_inc(w_lo, 1)

            def last(i, g, s, k):
                iteration(i, g, s, k, True)

            def iteration(i, g, s, k, last=False):
                for j in range(GH):
                    t = i * GH + j
                    if j == 1 and live(i - 2, ITERS):
                        v.wait_ge(pv_done, GH * (i - 1))
                        v.wait_ge(dv_done, i - 1)
                        at_least(v, y_out[k], 8 * (i - k) - 16)
                        v.tensor_tensor(yst[k][:], ps_y[k][0:GCH, 0:SEQ], dv[k][:], ALU.add).then_inc(yhi_done, 1)
                    if j == 2 and live(i - 2, ITERS):
                        v.wait_ge(ylo_done, i - 1)
                        v.wait_ge(yhi_done, i - 1)
                        v.tensor_tensor(yst[k][:], yst[k][:], y_lo[:], ALU.add).then_inc(y_evac, 1)
                    if live(t - 3, UNITS):
                        r = (j + 1) % 4
                        v.wait_ge(mh_done, t - 2)
                        at_least(v, pv_done, t - 6)
                        v.tensor_tensor(m_l[r][:], m_f[(j + 1) % 2][:], f32(m_h[r][:]), ALU.subtract
                                        ).then_inc(ml_done, 1)
                    if live(t - 2, UNITS):
                        r = (j + 2) % 4
                        kk = k if j >= 2 else 1 - k
                        n = i if j >= 2 else i - 1
                        v.wait_ge(c_done, t - 1)
                        v.wait_ge(hl_done, t - 1)
                        own = ps_c[j % 2][:, SEQ:LW]
                        v.tensor_tensor(own, own, hl[j % 2][:], ALU.add).then_inc(own_done, 1)
                        v.wait_ge(own_done, t - 1)
                        v.wait_ge(exp_done, n * 2 + r // 2 + 1)
                        v.tensor_tensor(m_f[j % 2][:], ps_c[j % 2][:, 0:LW], dec[kk][:, r, :], ALU.mult
                                        ).then_inc(mt_done, 1)
                    if live(i, ITERS):
                        v.wait_ge(bh_done, t + 1)
                        v.tensor_tensor(bc[j % 2][:, 1, :], ps_p[j][:], f32(bc[j % 2][:, 0, :]), ALU.subtract
                                        ).then_inc(bl_done, 1)
                        if last:
                            split_weights(g + 1, j)
            for j in range(GH):
                split_weights(0, j)
            walk(v, iteration, last=last)
            weights.split_lo(v)


class Weights:

    def __init__(self, sc, name, items):
        self.items = items
        self.raws = [sc.sb(f"{name}_{label}", list(hi.shape)) for label, hi, _, _ in items]
        self.loaded = [sc.sem(f"{name}_{label}_loaded") for label, _, _, _ in items]
        self.zeroed, self.hi_done, self.lo_done = (
            sc.sem(f"{name}_{n}") for n in ("zeroed", "hi_done", "lo_done"))

    def zero(self, pool):
        for raw in self.raws:
            pool.memset(raw[:], 0.0).then_inc(self.zeroed, 1)

    def load(self, sp):
        for i, (_, _, _, loads) in enumerate(self.items):
            sp.wait_ge(self.zeroed, i + 1)
            for where, src in loads:
                sp.dma_start(self.raws[i][where], src).then_inc(self.loaded[i], 16)

    def split_hi(self, act, first=0, end=None):
        for i, (_, hi, _, loads) in list(enumerate(self.items))[first:end]:
            act.wait_ge(self.loaded[i], 16 * len(loads))
            act.activation(hi[:], self.raws[i][:], ACT.Copy).then_inc(self.hi_done, 1)

    def split_lo(self, eng):
        for i, (_, hi, lo, _) in enumerate(self.items):
            eng.wait_ge(self.hi_done, i + 1)
            eng.tensor_tensor(lo[:], self.raws[i][:], f32(hi[:]), ALU.subtract).then_inc(self.lo_done, 1)


def stage_mixer_out(nc, d, keep):
    with ExitStack() as ctx:
        sc = Scope(nc, ctx, "out")
        x_sb, mean, rstd, xh, xl = (keep[n] for n in ("x", "mean", "rstd", "xh", "xl"))
        wg_h, wg_l = keep["wg_h"], keep["wg_l"]
        wo_h, wo_l = (sc.sb(n, [P, CT, DM], F32R) for n in ("wo_h", "wo_l"))
        every = (slice(None), slice(None), slice(None))
        weights = Weights(sc, "w", [("out", wo_h, wo_l, [(every, d["w_out"])])])
        st = sc.sb("st", [P, TILES, 6])
        yb = [sc.sb(f"yb{k}", [P, CT, BLK]) for k in range(2)]
        sg = [sc.sb(f"sg{ct}", [P, BLK]) for ct in range(CT)]
        u_h = [sc.sb(f"u_h{k}", [P, CT, BLK], F32R) for k in range(2)]
        u_l = [sc.sb(f"u_l{k}", [P, CT, BLK], F32R) for k in range(2)]
        ps_g = [sc.bank(f"ps_g{ct}") for ct in range(CT)]
        ps_o = [sc.bank(f"ps_o{b}") for b in range(2)]
        y_in = [sc.sem(f"y_in{k}") for k in range(2)]
        g_done, sg_done, u_done, uh_done, ul_done = (
            sc.sem(n) for n in ("g_done", "sg_done", "u_done", "uh_done", "ul_done"))
        o_done, x_done, stats_done, step, var_ready, root_done, rstd_done, x_out = (
            sc.sem(n) for n in ("o_done", "x_done", "stats_done", "step", "var_ready", "root_done",
                                "rstd_done", "x_out"))
        block = ctx.enter_context(nc.Block())

        def slots(eng, slot):
            for n in range(2):
                slot(n, n % 2)
            with eng.Fori(1, NBLK // 2) as q:
                for k in range(2):
                    slot(q * 2 + k, k)
            for n in range(NBLK, NBLK + 2):
                slot(n, n % 2)

        def live(n):
            return not isinstance(n, int) or 0 <= n < NBLK

        @block.sync
        def _(sp):
            weights.load(sp)
            y_view = d["y"].rearrange("(c f s) r l -> f r c s l", c=CT, f=2)

            def slot(n, k):
                if live(n):
                    at_least(sp, ul_done, CT * (n - 1))
                    for half in range(2):
                        rows = slice(half * GCH, (half + 1) * GCH)
                        for ct in range(CT):
                            sp.dma_start(yb[k][rows, ct, :].rearrange("p (s l) -> p s l", l=SEQ),
                                         y_view[half, :, ct, bass.ds(n * 2, 2), :]).then_inc(y_in[k], 16)
                if live(n - 2):
                    sp.wait_ge(x_done, 2 * (n - 1))
                    sp.dma_start(d["x1"][:, bass.ds((n - 2) * TPB, TPB), :],
                                 x_sb[:, bass.ds((n - 2) * TPB, TPB), :]).then_inc(x_out, 16)
            slots(sp, slot)
            sp.wait_ge(x_out, 16 * NBLK)

        @block.tensor
        def _(pe):
            def slot(n, k):
                m = n - 1
                if live(n):
                    for ct in range(CT):
                        at_least(pe, sg_done, CT * (n - 1) + ct + 1)
                        for kt in range(KT):
                            last = three_passes(pe, ps_g[ct][:], wg_h[:, kt, ct * P:(ct + 1) * P],
                                                wg_l[:, kt, ct * P:(ct + 1) * P],
                                                xh[:, kt, bass.ds(n * BLK, BLK)], xl[:, kt, bass.ds(n * BLK, BLK)],
                                                kt == 0, kt == KT - 1)
                        last.then_inc(g_done, 1)
                if live(m):
                    if isinstance(n, int) and n == 1:
                        pe.wait_ge(weights.lo_done, 1)
                    pe.wait_ge(ul_done, CT * n)
                    for b in range(2):
                        at_least(pe, x_done, 2 * (m - 1) + b + 1)
                        for q in (2 * b, 2 * b + 1):
                            tok = slice(q * P, (q + 1) * P)
                            for ct in range(CT):
                                last = three_passes(pe, ps_o[b][:, (q % 2) * DM:(q % 2 + 1) * DM],
                                                    u_h[1 - k][:, ct, tok], u_l[1 - k][:, ct, tok],
                                                    wo_h[:, ct, :], wo_l[:, ct, :], ct == 0, ct == CT - 1)
                        last.then_inc(o_done, 1)
            slots(pe, slot)

        @block.scalar
        def _(act):
            weights.split_hi(act)

            def slot(n, k):
                if live(n):
                    for ct in range(CT):
                        act.wait_ge(g_done, CT * n + ct + 1)
                        at_least(act, u_done, CT * (n - 1) + ct + 1)
                        act.activation(sg[ct][:], ps_g[ct][:], ACT.Silu).then_inc(sg_done, 1)
                    for ct in range(CT):
                        act.wait_ge(u_done, CT * n + ct + 1)
                        at_least(act, o_done, 2 * (n - 1))
                        act.activation(u_h[k][:, ct, :], yb[k][:, ct, :], ACT.Copy).then_inc(uh_done, 1)
            slots(act, slot)
            act.wait_ge(var_ready, 1)
            act.activation(rstd[:], rstd[:], ACT.Sqrt).then_inc(root_done, 1)

        @block.gpsimd
        def _(pool):
            weights.zero(pool)

            def slot(n, k):
                if live(n):
                    pool.wait_ge(y_in[k], 64 * (n - k) + 128)
                    for ct in range(CT):
                        pool.wait_ge(sg_done, CT * n + ct + 1)
                        pool.tensor_tensor(yb[k][:, ct, :], yb[k][:, ct, :], sg[ct][:], ALU.mult
                                           ).then_inc(u_done, 1)
            slots(pool, slot)

        @block.vector
        def _(v):
            weights.split_lo(v)

            def slot(n, k):
                m = n - 1
                if live(n):
                    for ct in range(CT):
                        v.wait_ge(uh_done, CT * n + ct + 1)
                        v.tensor_tensor(u_l[k][:, ct, :], yb[k][:, ct, :], f32(u_h[k][:, ct, :]), ALU.subtract
                                        ).then_inc(ul_done, 1)
                if live(m):
                    for b in range(2):
                        v.wait_ge(o_done, 2 * m + b + 1)
                        two = bass.ds(m * TPB + 2 * b, 2)
                        v.tensor_tensor(x_sb[:, two, :], ps_o[b][:].rearrange("p (q d) -> p q d", q=2),
                                        x_sb[:, two, :], ALU.add).then_inc(x_done, 1)
                    for q in range(TPB):
                        v.wait_ge(x_done, 2 * m + q // 2 + 1)
                        one = bass.ds(m * TPB + q, 1)
                        v.bn_stats(st[:, one, :].rearrange("p o s -> p (o s)"),
                                   x_sb[:, one, :].rearrange("p o d -> p (o d)")).then_inc(stats_done, 1)
            slots(v, slot)
            finish_moments(v, st, mean, rstd, stats_done, step, var_ready, root_done, rstd_done)


def stage_route(nc, d, keep, expert_weights):
    with ExitStack() as ctx:
        sc = Scope(nc, ctx, "rt")
        x_sb, mean, rstd = keep["x"], keep["mean"], keep["rstd"]
        wr_h, wr_l = (sc.sb(n, [P, KT, P], F32R) for n in ("wr_h", "wr_l"))
        weights = Weights(sc, "w", [("route", wr_h, wr_l, [((slice(None), slice(None), slice(0, E)), d["w_route"])])]
                          + expert_weights)
        ident = sc.sb("ident", [P, P])
        rank = sc.sb("rank", [P, E])
        xn = [sc.sb(f"xn{k}", [P, TPB, DM]) for k in range(2)]
        x2h = [sc.sb(f"x2h{k}", [P, KT, BLK], F32R) for k in range(2)]
        x2l = [sc.sb(f"x2l{k}", [P, KT, BLK], F32R) for k in range(2)]
        lgT = [sc.sb(f"lgT{k}", [P, BLK]) for k in range(2)]
        lg = sc.sb("lg", [P, TILES, E])
        cand = sc.sb("cand", [P, TILES, E])
        best = sc.sb("best", [P, TILES])
        top = sc.sb("top", [P, CPS, 2, SEQS])
        hot = sc.sb("hot", [P, TILES, 2, E])
        hotT = sc.sb("hotT", [P, 4, P])
        mx, tot, inv = (sc.sb(n, [2 * SEQS, 1]) for n in ("mx", "tot", "inv"))
        soft = sc.sb("soft", [2 * SEQS, SEQ])
        ps_t = [[sc.bank(f"ps_t{k}{kt}") for kt in range(KT)] for k in range(2)]
        ps_l = sc.bank("ps_l")
        ps_lt = sc.bank("ps_lt")
        ps_top, ps_hot = sc.bank("ps_top"), sc.bank("ps_hot")
        small_in = sc.sem("small_in")
        xn_ready, tr_done, hi_done, lo_done, l_done, lT_done, lt_done, lg_done = (
            sc.sem(n) for n in ("xn_ready", "tr_done", "hi_done", "lo_done", "l_done", "lT_done",
                                "lt_done", "lg_done"))
        x2_out = [sc.sem(f"x2_out{k}") for k in range(2)]
        step, top_done, topT_done, mx_done, soft_exp, soft_done, hotT_done, hot_copied, out = (
            sc.sem(n) for n in ("step", "top_done", "topT_done", "mx_done", "soft_exp", "soft_done",
                                "hotT_done", "hot_copied", "out"))
        block = ctx.enter_context(nc.Block())

        def slots(eng, slot, side=None):
            for n in range(2):
                slot(n, n % 2)
            if side:
                side(1, 5)
            with eng.Fori(1, NBLK // 2 - 1) as q:
                for k in range(2):
                    slot(q * 2 + k, k)
            if side:
                side(5, 8)
            for n in range(NBLK - 2, NBLK + 2):
                slot(n, n % 2)
                if side and n == NBLK - 2:
                    side(8, None)

        def live(n):
            return not isinstance(n, int) or 0 <= n < NBLK

        @block.sync
        def _(sp):
            sp.dma_start(ident[:], d["ident"]).then_inc(small_in, 16)
            sp.dma_start(rank[:], d["rank"]).then_inc(small_in, 16)
            weights.load(sp)

            def slot(n, k):
                if live(n):
                    sp.wait_ge(hi_done, n + 1)
                    sp.dma_start(d["x2h"][bass.ds(n, 1)].rearrange("n p k l -> p (n k) l"), f32(x2h[k][:])
                                 ).then_inc(x2_out[k], 16)
                    sp.wait_ge(lo_done, n + 1)
                    sp.dma_start(d["x2l"][bass.ds(n, 1)].rearrange("n p k l -> p (n k) l"), f32(x2l[k][:])
                                 ).then_inc(x2_out[k], 16)
            slots(sp, slot)
            sp.wait_ge(hot_copied, 1)
            for b in range(4):
                sp.dma_start(d["hot"][:, b * 8 * P:(b + 1) * 8 * P].rearrange("q (t l) -> t q l", t=8),
                             hotT[:, b, :]).then_inc(out, 16)
            sp.wait_ge(soft_done, 1)
            sp.dma_start(d["soft"].rearrange("r (s l) -> (r s) l", l=SEQ), soft[:]).then_inc(out, 16)
            sp.wait_ge(out, 5 * 16)
            for k in range(2):
                sp.wait_ge(x2_out[k], 32 * (NBLK // 2))

        @block.tensor
        def _(pe):
            pe.wait_ge(small_in, 32)

            def slot(n, k):
                m, o = n - 1, n - 2
                if live(n):
                    pe.wait_ge(xn_ready, n + 1)
                    at_least(pe, lo_done, n - 1)
                    for kt in range(KT):
                        for q in range(TPB):
                            last = pe.transpose(ps_t[k][kt][:, q * P:(q + 1) * P],
                                                xn[k][:, q, kt * P:(kt + 1) * P], ident[:])
                    last.then_inc(tr_done, 1)
                if live(m):
                    if isinstance(n, int) and n == 1:
                        pe.wait_ge(weights.lo_done, 1)
                    pe.wait_ge(lo_done, m + 1)
                    at_least(pe, lT_done, m)
                    for kt in range(KT):
                        last = three_passes(pe, ps_l[:], wr_h[:, kt, :], wr_l[:, kt, :],
                                            x2h[1 - k][:, kt, :], x2l[1 - k][:, kt, :], kt == 0, kt == KT - 1)
                    last.then_inc(l_done, 1)
                if live(o):
                    pe.wait_ge(lT_done, o + 1)
                    at_least(pe, lg_done, o)
                    for q in range(TPB):
                        last = pe.transpose(ps_lt[:, q * P:(q + 1) * P], lgT[k][:, q * P:(q + 1) * P], ident[:])
                    last.then_inc(lt_done, 1)
            slots(pe, slot)
            pe.wait_ge(top_done, 2)
            for c in range(CPS):
                last = pe.transpose(ps_top[0:2 * SEQS, c * P:(c + 1) * P],
                                    top[:, c, :, :].rearrange("p r s -> p (r s)"), ident[:])
            last.then_inc(topT_done, 1)
            pe.wait_ge(step, 11)
            for b in range(4):
                last = pe.transpose(ps_hot[:, b * P:(b + 1) * P],
                                    hot[:, b * 8:(b + 1) * 8, :, :].rearrange("p t r e -> p (t r e)"), ident[:])
            last.then_inc(hotT_done, 1)

        @block.gpsimd
        def _(pool):
            weights.zero(pool)
            weights.split_lo(pool)

        @block.scalar
        def _(act):
            weights.split_hi(act, 0, 1)

            def slot(n, k):
                m = n - 1
                if live(n):
                    act.wait_ge(tr_done, n + 1)
                    at_least(act, x2_out[k], 16 * (n - k))
                    at_least(act, l_done, n - 1)
                    for kt in range(KT):
                        last = act.activation(x2h[k][:, kt, :], ps_t[k][kt][:], ACT.Copy)
                    last.then_inc(hi_done, 1)
                if live(m):
                    act.wait_ge(l_done, m + 1)
                    at_least(act, lt_done, m - 1)
                    act.activation(lgT[1 - k][:], ps_l[:], ACT.Copy).then_inc(lT_done, 1)
            slots(act, slot, lambda first, end: weights.split_hi(act, first, end))
            act.wait_ge(mx_done, 1)
            act.activation(soft[:], ps_top[0:2 * SEQS, 0:SEQ], ACT.Exp, bias=mx[:, 0:1],
                           accum_out=tot[:, 0:1]).then_inc(soft_exp, 1)
            act.wait_ge(hotT_done, 1)
            act.activation(hotT[:].rearrange("p b l -> p (b l)"), ps_hot[:], ACT.Copy).then_inc(hot_copied, 1)

        @block.vector
        def _(v):
            v.wait_ge(small_in, 32)

            def normalise(n, k):
                at_least(v, tr_done, n - 1)
                for q in range(TPB):
                    t = n * TPB + q
                    last = v.tensor_scalar(xn[k][:, q, :], x_sb[:, bass.ds(t, 1), :], mean[:, bass.ds(t, 1)],
                                           rstd[:, bass.ds(t, 1)], ALU.subtract, ALU.mult)
                last.then_inc(xn_ready, 1)

            def slot(n, k):
                o = n - 2
                if live(n + 1):
                    normalise(n + 1, 1 - k)
                if live(n):
                    v.wait_ge(hi_done, n + 1)
                    for kt in range(KT):
                        last = v.tensor_tensor(x2l[k][:, kt, :], ps_t[k][kt][:], f32(x2h[k][:, kt, :]), ALU.subtract)
                    last.then_inc(lo_done, 1)
                if live(o):
                    v.wait_ge(lt_done, o + 1)
                    v.tensor_copy(lg[:, bass.ds(o * TPB, TPB), :],
                                  ps_lt[:].rearrange("p (q e) -> p q e", q=TPB)[:, :, 0:E]).then_inc(lg_done, 1)
            normalise(0, 0)
            slots(v, slot)
            v.wait_ge(lg_done, NBLK)
            wide = [P, TILES, E]
            steps = 0
            for r in range(2):
                v.tensor_reduce(best[:], lg[:], AX_X, ALU.max).then_inc(step, 1)
                steps += 1
                v.wait_ge(step, steps)
                v.tensor_copy(top[:, :, r, :].rearrange("p c s -> p s c"),
                              best[:].rearrange("p (s c) -> p s c", c=CPS)).then_inc(top_done, 1)
                v.tensor_tensor(cand[:], lg[:], best[:].unsqueeze(2).broadcast_to(wide), ALU.is_equal
                                ).then_inc(step, 1)
                steps += 1
                v.wait_ge(step, steps)
                v.tensor_tensor(cand[:], cand[:], rank[:].unsqueeze(1).broadcast_to(wide), ALU.mult).then_inc(step, 1)
                steps += 1
                v.wait_ge(step, steps)
                v.wait_ge(top_done, r + 1)
                v.tensor_reduce(best[:], cand[:], AX_X, ALU.max).then_inc(step, 1)
                steps += 1
                v.wait_ge(step, steps)
                v.tensor_tensor(hot[:, :, r, :], cand[:], best[:].unsqueeze(2).broadcast_to(wide), ALU.is_equal
                                ).then_inc(step, 1)
                steps += 1
                v.wait_ge(step, steps)
                if r == 0:
                    v.scalar_tensor_tensor(lg[:], hot[:, :, 0, :], -3.0e38, lg[:], ALU.mult, ALU.add
                                           ).then_inc(step, 1)
                    steps += 1
                    v.wait_ge(step, steps)
            v.wait_ge(topT_done, 1)
            v.tensor_reduce(mx[:], ps_top[0:2 * SEQS, 0:SEQ], AX_X, ALU.max).then_inc(step, 1)
            v.wait_ge(step, steps + 1)
            v.tensor_scalar(mx[:], mx[:], -1.0, None, ALU.mult).then_inc(mx_done, 1)
            v.wait_ge(soft_exp, 1)
            v.reciprocal(inv[:], tot[:]).then_inc(step, 1)
            v.wait_ge(step, steps + 2)
            v.tensor_scalar(soft[:], soft[:], inv[:, 0:1], None, ALU.mult).then_inc(soft_done, 1)


EXPERT_WEIGHTS = (("au", [KT, P]), ("ag", [KT, P]), ("wu", [KT, HP]), ("wg", [KT, HP]), ("bu", [HP]), ("bg", [HP]),
                  ("da", [HT, P]), ("wd", [HT, DM]), ("db", [DM]))


def expert_weights(xh, xl, d):
    w, at = {}, 0
    for name, shape in EXPERT_WEIGHTS:
        size = math.prod(shape)
        for part, place in (("h", xh), ("l", xl)):
            tile = place[:].rearrange("p k t -> p (k t)")[:, at:at + size]
            if len(shape) == 2:
                tile = tile.rearrange("p (a b) -> p a b", a=shape[0])
            w[f"{name}_{part}"] = tile
        at += size
    al = slice(None)

    def by_tiles(src):
        full = HID // P
        return [((al, slice(0, full), al), src[0:full * P, :].rearrange("(t p) n -> p t n", p=P)),
                ((slice(0, HID - full * P), full, al), src[full * P:HID, :])]

    loads = {"au": [((al, al, al), d["up_a"])],
             "ag": [((al, al, al), d["gate_a"])],
             "wu": [((al, al, slice(0, HID)), d["w_up"])],
             "wg": [((al, al, slice(0, HID)), d["w_gate2"])],
             "bu": [((al, slice(0, HID)), d["up_b"])],
             "bg": [((al, slice(0, HID)), d["gate_b"])],
             "da": by_tiles(d["down_a"]),
             "wd": by_tiles(d["w_down"]),
             "db": [((al, al), d["down_b"])]}
    return w, [(n, w[n + "_h"], w[n + "_l"], loads[n]) for n, _ in EXPERT_WEIGHTS]


def stage_experts(nc, d, w):
    with ExitStack() as ctx:
        sc = Scope(nc, ctx, "ffn")
        (wu_h, wu_l, wg_h, wg_l, bu_h, bu_l, bg_h, bg_l, wd_h, wd_l, da_h, da_l, au_h, au_l, ag_h, ag_l,
         db_h, db_l) = (w[n] for n in ("wu_h", "wu_l", "wg_h", "wg_l", "bu_h", "bu_l", "bg_h", "bg_l",
                                       "wd_h", "wd_l", "da_h", "da_l", "au_h", "au_l", "ag_h", "ag_l",
                                       "db_h", "db_l"))
        x2h = [sc.sb(f"x2h{k}", [P, KT, BLK], F32R) for k in range(2)]
        x2l = [sc.sb(f"x2l{k}", [P, KT, BLK], F32R) for k in range(2)]
        msk = [sc.sb(f"msk{k}", [P, 2, BLK]) for k in range(2)]
        mdif = sc.sb("mdif", [P, BLK])
        wbc = [sc.sb(f"wbc{k}", [P, 2, BLK]) for k in range(2)]
        xo = [sc.sb(f"xo{k}", [P, TPB, DM]) for k in range(2)]
        am_h = [sc.sb(f"am_h{k}", [P, 4, BLK], F32R) for k in range(2)]
        am_l = [sc.sb(f"am_l{k}", [P, 4, BLK], F32R) for k in range(2)]
        am_f = [sc.sb(f"am_f{k}", [P, BLK]) for k in range(2)]
        ch_f = [[sc.sb(f"ch_f{r}{j}", [P, BLK]) for j in range(2)] for r in range(2)]
        ch_h = [[sc.sb(f"ch_h{r}{j}", [P, BLK], F32R) for j in range(2)] for r in range(2)]
        ch_l = [[sc.sb(f"ch_l{r}{j}", [P, BLK], F32R) for j in range(2)] for r in range(2)]
        mix_f = [sc.sb(f"mix_f{j}", [P, BLK]) for j in range(4)]
        mix_h, mix_l = (sc.sb(n, [P, HT, BLK], F32R) for n in ("mix_h", "mix_l"))
        z_f = [sc.sb(f"z_f{r}", [P, BLK]) for r in range(2)]
        z_h, z_l = sc.sb("z_h", [P, BLK], F32R), sc.sb("z_l", [P, BLK], F32R)
        ps_u = [sc.bank(f"ps_u{j}") for j in range(2)]
        ps_g = [sc.bank(f"ps_g{j}") for j in range(2)]
        ps_d = [sc.bank(f"ps_d{r}") for r in range(2)]
        ps_a = [sc.bank(f"ps_a{b}") for b in range(2)]
        x2_in, msk_in, w_in, x1_in, out_done = (
            [sc.sem(f"{n}{k}") for k in range(2)] for n in ("x2_in", "msk_in", "w_in", "x1_in", "out_done"))
        ax_done, mdif_done, amf_done, amh_done, aml_done = (
            sc.sem(n) for n in ("ax_done", "mdif_done", "amf_done", "amh_done", "aml_done"))
        ug0_done, ug1_done, s0_done, s1_done, p0_done, p1_done = (
            sc.sem(n) for n in ("ug0_done", "ug1_done", "s0_done", "s1_done", "p0_done", "p1_done"))
        chf_done, chh_done, chl_done, mixf_done, mixh_done, mixl_done, da_done = (
            sc.sem(n) for n in ("chf_done", "chh_done", "chl_done", "mixf_done", "mixh_done", "mixl_done",
                                "da_done"))
        zp_done, zf_done, zh_done, zl_done, fin_done, fin_evac = (
            sc.sem(n) for n in ("zp_done", "zf_done", "zh_done", "zl_done", "fin_done", "fin_evac"))
        STEPS = NBLK * HT
        block = ctx.enter_context(nc.Block())

        def mix_slot(h, k):
            return (HT * k + h) % 4

        def walk(eng, step):
            def blocks(n, k):
                for h in range(HT):
                    step(n, h, k)
            for n in range(2):
                blocks(n, n % 2)
            with eng.Fori(1, NBLK // 2 - 1) as q:
                for k in range(2):
                    blocks(q * 2 + k, k)
            for n in range(NBLK - 2, NBLK + 1):
                blocks(n, n % 2)

        def live(n, end):
            return not isinstance(n, int) or 0 <= n < end

        @block.sync
        def _(sp):
            def load(n, k):
                cols = bass.ds(n * BLK, BLK)
                at_least(sp, ug0_done, HT * (n - 1))
                for dst, src in ((x2h, "x2h"), (x2l, "x2l")):
                    sp.dma_start(f32(dst[k][:]), d[src][bass.ds(n, 1)].rearrange("n p k l -> p (n k) l")
                                 ).then_inc(x2_in[k], 16)
                at_least(sp, zp_done, 2 * (n - 1))
                for r in range(2):
                    sp.dma_start(msk[k][:, r, :], d["hot"][r * E:(r + 1) * E, cols].unsqueeze(1)
                                 .broadcast_to([E, R, BLK])).then_inc(msk_in[k], 16)
                at_least(sp, chf_done, 2 * HT * (n - 1))
                sp.dma_start(wbc[k][:], d["soft"][:, cols].partition_broadcast(P)).then_inc(w_in[k], 16)

            def store(n, k):
                for b in range(2):
                    sp.wait_ge(fin_evac, 2 * n + b + 1)
                    sp.dma_start(d["out"][bass.ds(n * 2 + b, 1)].rearrange("s (c p) d -> p (s c) d", p=P),
                                 xo[k][:, 2 * b:2 * b + 2, :]).then_inc(out_done[k], 16)

            def load_x1(n, k):
                at_least(sp, out_done[k], 16 * (n - k))
                sp.dma_start(xo[k][:], d["x1"][:, bass.ds(n * TPB, TPB), :]).then_inc(x1_in[k], 16)

            for n in range(2):
                load(n, n)
                load_x1(n, n)
            for n in range(2, 4):
                load(n, n % 2)
                store(n - 2, n % 2)
                load_x1(n, n % 2)
            with sp.Fori(2, NBLK // 2) as q:
                for k in range(2):
                    n = q * 2 + k
                    load(n, k)
                    store(n - 2, k)
                    load_x1(n, k)
            for n in range(NBLK - 2, NBLK):
                store(n, n % 2)
            for k in range(2):
                sp.wait_ge(out_done[k], 16 * NBLK)

        @block.tensor
        def _(pe):
            def a_x(n, k):
                pe.wait_ge(x2_in[k], 16 * (n - k) + 32)
                for b, (w_h, w_l) in enumerate(((au_h, au_l), (ag_h, ag_l))):
                    at_least(pe, fin_evac, 2 * (n - 2) + b + 1)
                    at_least(pe, amf_done, 4 * n)
                    for kt in range(KT):
                        last = three_passes(pe, ps_a[b][:], w_h[:, kt, :], w_l[:, kt, :],
                                            x2h[k][:, kt, :], x2l[k][:, kt, :], kt == 0, kt == KT - 1)
                    last.then_inc(ax_done, 1)

            def output(n, k):
                pe.wait_ge(mixl_done, HT * (n + 1))
                pe.wait_ge(zl_done, n + 1)
                for b in range(2):
                    for q in (2 * b, 2 * b + 1):
                        tok = slice(q * P, (q + 1) * P)
                        out = ps_a[b][:, (q % 2) * DM:(q % 2 + 1) * DM]
                        for h in range(HT):
                            three_passes(pe, out, mix_h[:, h, tok], mix_l[:, h, tok],
                                         wd_h[:, h, :], wd_l[:, h, :], h == 0, False)
                        last = three_passes(pe, out, z_h[:, tok], z_l[:, tok], db_h[:], db_l[:], False, True)
                    last.then_inc(fin_done, 1)

            def step(n, h, k):
                c = n * HT + h
                if h == 4 and live(n - 1, NBLK):
                    if live(n, NBLK):
                        pe.wait_ge(amf_done, 4 * (n + 1))
                    output(n - 1, 1 - k)
                if h == 5 and live(n + 1, NBLK):
                    a_x(n + 1, 1 - k)
                hid = slice(h * P, (h + 1) * P)
                if live(c, STEPS):
                    j = h % 2
                    for out, w_h, w_l, b_h, b_l, a, read in (
                            (ps_u[j], wu_h, wu_l, bu_h, bu_l, 0, s1_done),
                            (ps_g[j], wg_h, wg_l, bg_h, bg_l, 1, p1_done)):
                        at_least(pe, read, c - 1)
                        for kt in range(KT):
                            three_passes(pe, out[:], w_h[:, kt, hid], w_l[:, kt, hid],
                                         x2h[k][:, kt, :], x2l[k][:, kt, :], kt == 0, False)
                        pe.wait_ge(aml_done, 4 * n + a + 1)
                        last = three_passes(pe, out[:], b_h[:, hid], b_l[:, hid],
                                            am_h[k][:, a, :], am_l[k][:, a, :], False, True)
                    last.then_inc(ug0_done, 1)
                if live(c - 1, STEPS):
                    hh = (h - 1) % HT
                    nn, kk = (n, k) if h >= 1 else (n - 1, 1 - k)
                    prev = slice(hh * P, (hh + 1) * P)
                    pe.wait_ge(p0_done, c)
                    pe.wait_ge(aml_done, 4 * (nn + 1))
                    for out, b_h, b_l, a in ((ps_u[hh % 2], bu_h, bu_l, 2), (ps_g[hh % 2], bg_h, bg_l, 3)):
                        last = three_passes(pe, out[:], b_h[:, prev], b_l[:, prev],
                                            am_h[kk][:, a, :], am_l[kk][:, a, :], False, True, True)
                    last.then_inc(ug1_done, 1)
                if live(c - 2, STEPS):
                    hh = (h - 2) % HT
                    nn = n if h >= 2 else n - 1
                    if hh == 0:
                        at_least(pe, zp_done, 2 * nn)
                    for r in range(2):
                        pe.wait_ge(chl_done, 2 * (c - 2) + r + 1)
                        last = three_passes(pe, ps_d[r][:], da_h[:, hh, :], da_l[:, hh, :],
                                            ch_h[r][hh % 2][:], ch_l[r][hh % 2][:], hh == 0, hh == HT - 1)
                    last.then_inc(da_done, 1)

            a_x(0, 0)
            walk(pe, step)

        @block.scalar
        def _(act):
            def split_am(n, k, parts):
                for a in parts:
                    act.wait_ge(amf_done, 4 * n + a + 1)
                    at_least(act, ug1_done, HT * (n - 1))
                    act.activation(am_h[k][:, a, :], am_f[a % 2][:], ACT.Copy).then_inc(amh_done, 1)

            def step(n, h, k):
                c = n * HT + h
                j = h % 2
                if live(c - 2, STEPS):
                    for r in range(2):
                        act.wait_ge(chf_done, 2 * (c - 2) + r + 1)
                        at_least(act, da_done, c - 3)
                        act.activation(ch_h[r][j][:], ch_f[r][j][:], ACT.Copy).then_inc(chh_done, 1)
                if h == 3 and live(n - 1, NBLK):
                    act.wait_ge(zf_done, n)
                    at_least(act, fin_done, 2 * (n - 1))
                    act.activation(z_h[:], z_f[0][:], ACT.Copy).then_inc(zh_done, 1)
                if h == 5 and live(n + 1, NBLK):
                    split_am(n + 1, 1 - k, (0, 1))
                if h == 0 and live(n, NBLK):
                    split_am(n, k, (2, 3))
                if live(c - 4, STEPS):
                    hh = (h - 4) % HT
                    nn = n if h >= 4 else n - 1
                    act.wait_ge(mixf_done, c - 3)
                    at_least(act, fin_done, 2 * nn)
                    act.activation(mix_h[:, hh, :], mix_f[mix_slot(h, k)][:], ACT.Copy).then_inc(mixh_done, 1)
                if live(c, STEPS):
                    act.wait_ge(ug0_done, c + 1)
                    at_least(act, chl_done, 2 * (c - 1))
                    at_least(act, mixf_done, c - 1)
                    act.activation(ch_f[0][j][:], ps_u[j][:], ACT.Silu).then_inc(s0_done, 1)
                if live(c - 1, STEPS):
                    act.wait_ge(ug1_done, c)
                    act.activation(ch_f[1][1 - j][:], ps_u[1 - j][:], ACT.Silu).then_inc(s1_done, 1)

            split_am(0, 0, (0, 1))
            walk(act, step)

        @block.gpsimd
        def _(pool):
            def mask_difference(n, k):
                pool.wait_ge(msk_in[k], 16 * (n - k) + 32)
                at_least(pool, amf_done, 4 * n)
                pool.tensor_tensor(mdif[:], msk[k][:, 1, :], msk[k][:, 0, :], ALU.subtract
                                   ).then_inc(mdif_done, 1)

            def step(n, h, k):
                c = n * HT + h
                if h == 2 and live(n - 1, NBLK):
                    pool.wait_ge(zp_done, 2 * n)
                    pool.tensor_tensor(z_f[0][:], z_f[0][:], z_f[1][:], ALU.add).then_inc(zf_done, 1)
                if h == 4 and live(n + 1, NBLK):
                    mask_difference(n + 1, 1 - k)
                if live(c - 1, STEPS):
                    j = (h - 1) % 2
                    kk = k if h >= 1 else 1 - k
                    nn = n if h >= 1 else n - 1
                    if h == 1:
                        pool.wait_ge(w_in[kk], 8 * (nn - kk) + 16)
                    for r, done in ((0, p0_done), (1, p1_done)):
                        pool.wait_ge(done, c)
                        pool.tensor_tensor(ch_f[r][j][:], ch_f[r][j][:], wbc[kk][:, r, :], ALU.mult
                                           ).then_inc(chf_done, 1)
                    pool.wait_ge(chf_done, 2 * c)
                    at_least(pool, mixl_done, c - 4)
                    pool.tensor_tensor(mix_f[(mix_slot(h, k) - 1) % 4][:], ch_f[0][j][:], ch_f[1][j][:], ALU.add
                                       ).then_inc(mixf_done, 1)

            mask_difference(0, 0)
            walk(pool, step)

        @block.vector
        def _(v):
            def masked_ax(n, k, parts):
                for a in parts:
                    b = a % 2
                    mask = msk[k][:, 0, :] if a < 2 else mdif[:]
                    v.wait_ge(ax_done, 2 * n + b + 1)
                    at_least(v, aml_done, 4 * n + a - 1)
                    v.scalar_tensor_tensor(am_f[b][:], ps_a[b][:], LORA_ALPHA, mask, ALU.mult, ALU.mult
                                           ).then_inc(amf_done, 1)
                for a in parts:
                    v.wait_ge(amh_done, 4 * n + a + 1)
                    v.tensor_tensor(am_l[k][:, a, :], am_f[a % 2][:], f32(am_h[k][:, a, :]), ALU.subtract
                                    ).then_inc(aml_done, 1)

            def step(n, h, k):
                c = n * HT + h
                j = h % 2
                if live(c - 2, STEPS):
                    for r in range(2):
                        v.wait_ge(chh_done, 2 * (c - 2) + r + 1)
                        v.tensor_tensor(ch_l[r][j][:], ch_f[r][j][:], f32(ch_h[r][j][:]), ALU.subtract
                                        ).then_inc(chl_done, 1)
                if h == 2 and live(n - 1, NBLK):
                    m, kk = n - 1, 1 - k
                    v.wait_ge(da_done, HT * n)
                    at_least(v, zl_done, m)
                    for r in range(2):
                        v.scalar_tensor_tensor(z_f[r][:], ps_d[r][:], LORA_ALPHA, msk[kk][:, r, :], ALU.mult, ALU.mult
                                               ).then_inc(zp_done, 1)
                if h == 4 and live(n - 1, NBLK):
                    m, kk = n - 1, 1 - k
                    v.wait_ge(x1_in[kk], 8 * (m - kk) + 16)
                    for b in range(2):
                        v.wait_ge(fin_done, 2 * m + b + 1)
                        two = xo[kk][:, 2 * b:2 * b + 2, :]
                        v.tensor_tensor(two, ps_a[b][:].rearrange("p (q d) -> p q d", q=2), two, ALU.add
                                        ).then_inc(fin_evac, 1)
                if h == 5 and live(n + 1, NBLK):
                    v.wait_ge(msk_in[1 - k], 16 * (n + 1 - (1 - k)) + 32)
                    masked_ax(n + 1, 1 - k, (0, 1))
                if h == 0 and live(n, NBLK):
                    v.wait_ge(mdif_done, n + 1)
                    masked_ax(n, k, (2, 3))
                if h == 3 and live(n - 1, NBLK):
                    v.wait_ge(zh_done, n)
                    v.tensor_tensor(z_l[:], z_f[0][:], f32(z_h[:]), ALU.subtract).then_inc(zl_done, 1)
                if live(c - 4, STEPS):
                    hh = (h - 4) % HT
                    v.wait_ge(mixh_done, c - 3)
                    v.tensor_tensor(mix_l[:, hh, :], mix_f[mix_slot(h, k)][:], f32(mix_h[:, hh, :]), ALU.subtract
                                    ).then_inc(mixl_done, 1)
                if live(c, STEPS):
                    v.wait_ge(s0_done, c + 1)
                    v.tensor_tensor(ch_f[0][j][:], ps_g[j][:], ch_f[0][j][:], ALU.mult).then_inc(p0_done, 1)
                if live(c - 1, STEPS):
                    v.wait_ge(s1_done, c)
                    v.tensor_tensor(ch_f[1][1 - j][:], ps_g[1 - j][:], ch_f[1][1 - j][:], ALU.mult
                                    ).then_inc(p1_done, 1)

            v.wait_ge(msk_in[0], 32)
            masked_ax(0, 0, (0, 1))
            walk(v, step)


def program(nc, d):
    before = len(Scope.over)
    with ExitStack() as whole:
        sm = Scope(nc, whole, "m")
        keep = {"xh": sm.sb("xh", [P, KT, TOK], F32R), "xl": sm.sb("xl", [P, KT, TOK], F32R)}
        with ExitStack() as ctx:
            sc = Scope(nc, ctx, "k")
            keep.update(x=sc.sb("x", [P, TILES, DM]), mean=sc.sb("mean", [P, TILES]),
                        rstd=sc.sb("rstd", [P, TILES]))
            with ExitStack() as mix:
                keep["cumT"] = Scope(nc, mix, "c").sb("cumT", [P, TILES, H])
                with ExitStack() as early:
                    se = Scope(nc, early, "e")
                    keep["dt"] = se.sb("dt", [2 * H, TOK // 2])
                    keep["vs"] = [se.sb(f"vs{k}", [P, CT, SEQ]) for k in range(2)]
                    keep["vtok"] = [se.sb(f"vtok{k}", [P, CPS, DI]) for k in range(2)]
                    for n in ("wv_h", "wv_l"):
                        keep[n] = se.sb(n, [P, KT, DI + P], F32R)
                    stage_load_and_moments(nc, d, keep)
                    stage_values(nc, d, keep)
                    stage_decay(nc, d, keep)
                nc.clear_and_free_semaphores(Scope.over[before:])
                nc.all_engine_barrier()
                for n in ("wg_h", "wg_l"):
                    keep[n] = Scope(nc, mix, "g").sb(n, [P, KT, DI], F32R)
                stage_mixer(nc, d, keep)
                stage_mixer_out(nc, d, keep)
            w, items = expert_weights(keep["xh"], keep["xl"], d)
            stage_route(nc, d, keep, items)
        stage_experts(nc, d, w)


def kernel(**inputs):
    import numpy as np
    import concourse.bacc as bacc
    from concourse.bass_utils import run_bass_kernel_spmd

    a = {n[3:]: np.asarray(v) for n, v in inputs.items()}
    w = a["attn_W_in"]
    bc = w[2 * DI:2 * DI + 2 * H * N].reshape(2, H, N, KT, P)

    def by_k(m):
        return np.ascontiguousarray(m.T.reshape(-1, P, m.shape[0]).transpose(1, 0, 2))

    arrays = {
        "x": a["attn_x"],
        "w_val": by_k(w[:DI]),
        "w_gate": by_k(w[DI:2 * DI]),
        "w_dt": by_k(np.tile(w[2 * DI + 2 * H * N:], (2, 1))),
        "w_bc": np.ascontiguousarray(bc.transpose(1, 4, 3, 0, 2)).reshape(H, P, KT, 2 * N),
        "taps": np.ascontiguousarray(a["attn_conv_w"].reshape(CT, P, TAPS).transpose(1, 0, 2)),
        "conv_b": np.ascontiguousarray(a["attn_conv_b"].reshape(CT, P).T),
        "d_param": np.ascontiguousarray(a["attn_D_param"].reshape(GROUPS, GCH).T),
        "dt_bias": np.tile(a["attn_dt_bias"], 2).reshape(2 * H, 1),
        "a_log": np.tile(a["attn_A_log"], 2).reshape(2 * H, 1),
        "w_out": by_k(a["attn_W_out"]),
        "w_route": by_k(a["ffn_gate_w"]),
        "w_up": by_k(a["ffn_w_up"]),
        "w_gate2": by_k(a["ffn_w_gate"]),
        "w_down": np.ascontiguousarray(a["ffn_w_down"].T),
        "up_a": by_k(a["ffn_up_A"].reshape(E * R, DM)),
        "gate_a": by_k(a["ffn_gate_A"].reshape(E * R, DM)),
        "up_b": np.ascontiguousarray(a["ffn_up_B"].transpose(0, 2, 1).reshape(E * R, HID)),
        "gate_b": np.ascontiguousarray(a["ffn_gate_B"].transpose(0, 2, 1).reshape(E * R, HID)),
        "down_a": np.ascontiguousarray(a["ffn_down_A"].reshape(E * R, HID).T),
        "down_b": np.ascontiguousarray(a["ffn_down_B"].transpose(0, 2, 1).reshape(E * R, DM)),
        "ident": np.eye(P, dtype=np.float32),
        "rank": np.ascontiguousarray(np.broadcast_to(np.arange(E, 0, -1, dtype=np.float32), (P, E))),
        "mask": np.where(np.arange(P)[None, :] >= np.arange(P)[:, None], 0.0, NEG).astype(np.float32),
    }
    nc = bacc.Bacc("TRN2", target_bir_lowering=False, num_devices=1)
    d = {n: nc.dram_tensor(n, v.shape, mybir.dt.from_np(v.dtype), kind="ExternalInput").ap()
         for n, v in arrays.items()}
    for n, shape, dt in (("vT", [DI, TOK], F32), ("val", [SEQS, P, CPS, DI], F32),
                         ("cum", [H, TOK], F32), ("y", [GROUPS * SEQS, GCH, SEQ], F32), ("x1", [P, TILES, DM], F32),
                         ("x2h", [NBLK, P, KT, BLK], F32), ("x2l", [NBLK, P, KT, BLK], F32),
                         ("hot", [2 * E, TOK], F32), ("soft", [2, TOK], F32)):
        d[n] = nc.dram_tensor(f"{n}_scratch", shape, dt, kind="Internal").ap()
    d["out"] = nc.dram_tensor("out", [SEQS, SEQ, DM], F32, kind="ExternalOutput").ap()
    program(nc, d)
    r = run_bass_kernel_spmd(nc, [arrays], core_ids=[0])
    return r.results[0]["out"]
```
